# Optimizing a Trainium2 kernel written in Bass

```python
import numpy as np
import jax
import jax.numpy as jnp

def _softmax(x, axis=-1):
    return jax.nn.softmax(x, axis=axis)

def _gelu(x):
    return jax.nn.gelu(x, approximate=True)

def _silu(x):
    return jax.nn.silu(x)

def _sigmoid(x):
    return jax.nn.sigmoid(x)

def _layernorm(x, axis=-1, eps=1e-05):
    m = jnp.mean(x, axis=axis, keepdims=True)
    v = jnp.var(x, axis=axis, keepdims=True)
    return (x - m) / jnp.sqrt(v + eps)

def _scatter_add(tgt, idx, src, axis=0):
    return tgt.at[idx].add(src)

def _segment_sum(src, seg, n):
    return jax.ops.segment_sum(src, seg, n)
kernel_name = 'mk_gnn_ffn_d1_gnn_r8_95a2b8'

def setup_inputs(seed: int=0):
    np.random.seed(seed)
    _w = jnp.asarray

    def _rec_inputs():
        import jax
        import jax.numpy as jnp
        _gk = jax.random.key(seed)
        x = -0.0002117 + 1 * jax.random.normal(jax.random.fold_in(_gk, 1), (12500, 256), jnp.float32)
        src = jax.random.randint(jax.random.fold_in(_gk, 2), (200000,), 0, 12500, jnp.int32)
        dst = jax.random.randint(jax.random.fold_in(_gk, 3), (200000,), 0, 12500, jnp.int32)
        _o = jnp.argsort(dst, stable=True)
        src = src[_o]
        dst = dst[_o]
        edge_weight = jax.random.uniform(jax.random.fold_in(_gk, 12), (200000,), jnp.float32, 0.0, 1)
        return (x, src, dst, edge_weight)
    x, src, dst, edge_weight = _rec_inputs()

    def _L0_gnn_setup():
        import jax, jax.numpy as jnp
        import numpy as np
        N = 12500
        E = 400000
        DI = 256
        DO = 256
        BN_EPS = 1e-05

        def _bn_relu(h, gamma, beta):
            mean = jnp.mean(h, axis=0)
            var = jnp.var(h, axis=0)
            hn = (h - mean) * jax.lax.rsqrt(var + BN_EPS)
            return jax.nn.relu(hn * gamma + beta)
        key = jax.random.key(seed)
        ks = jax.random.split(key, 6)
        x = jax.random.normal(ks[0], (N, DI), dtype=jnp.float32)
        edge_row = jax.random.randint(ks[1], (E,), 0, N, dtype=jnp.int32)
        edge_col = jax.random.randint(ks[2], (E,), 0, N, dtype=jnp.int32)
        edge_vals = jnp.ones((E,), dtype=jnp.float32)
        eps = jnp.zeros((1,), dtype=jnp.float32)
        W1 = jax.random.normal(ks[3], (DI, DO), dtype=jnp.float32) * 0.05
        b1 = jnp.zeros((DO,), dtype=jnp.float32)
        g1 = jnp.ones((DO,), dtype=jnp.float32)
        be1 = jnp.zeros((DO,), dtype=jnp.float32)
        W2 = jax.random.normal(ks[4], (DO, DO), dtype=jnp.float32) * 0.05
        b2 = jnp.zeros((DO,), dtype=jnp.float32)
        g2 = jnp.ones((DO,), dtype=jnp.float32)
        be2 = jnp.zeros((DO,), dtype=jnp.float32)
        return {'x': x, 'edge_row': edge_row, 'edge_col': edge_col, 'edge_vals': edge_vals, 'eps': eps, 'W1': W1, 'b1': b1, 'g1': g1, 'be1': be1, 'W2': W2, 'b2': b2, 'g2': g2, 'be2': be2}
    _L0_gnn_all = _L0_gnn_setup()
    _L0_gnn_in = {k: v for k, v in _L0_gnn_all.items() if k in ('eps', 'W1', 'b1', 'g1', 'be1', 'W2', 'b2', 'g2', 'be2')}
    del _L0_gnn_all

    def _L0_ffn_setup():
        import jax, jax.numpy as jnp
        import numpy as np
        C = 256
        HID = 1024
        E = 8
        TEMP = 1.0
        key = jax.random.key(seed)
        ks = jax.random.split(key, 7)
        x = jax.random.normal(ks[0], (8, 2048, C), dtype=jnp.float32)
        W1 = jax.random.normal(ks[1], (C, HID), dtype=jnp.float32) * 0.02
        b1 = jnp.zeros((HID,), dtype=jnp.float32)
        Wg = jax.random.normal(ks[2], (HID, E), dtype=jnp.float32) * 0.02
        bg = jnp.zeros((E,), dtype=jnp.float32)
        Wd = jax.random.normal(ks[3], (E, HID, C), dtype=jnp.float32) * 0.02
        bd = jnp.zeros((E, C), dtype=jnp.float32)
        return {'x': x, 'W1': W1, 'b1': b1, 'Wg': Wg, 'bg': bg, 'Wd': Wd, 'bd': bd}
    _L0_ffn_all = _L0_ffn_setup()
    _L0_ffn_in = {k: v for k, v in _L0_ffn_all.items() if k in ('W1', 'b1', 'Wg', 'bg', 'Wd', 'bd')}
    del _L0_ffn_all
    return {'x': x, 'src': src, 'dst': dst, 'edge_weight': edge_weight, 'L0_gnn_eps': _L0_gnn_in['eps'], 'L0_gnn_W1': _L0_gnn_in['W1'], 'L0_gnn_b1': _L0_gnn_in['b1'], 'L0_gnn_g1': _L0_gnn_in['g1'], 'L0_gnn_be1': _L0_gnn_in['be1'], 'L0_gnn_W2': _L0_gnn_in['W2'], 'L0_gnn_b2': _L0_gnn_in['b2'], 'L0_gnn_g2': _L0_gnn_in['g2'], 'L0_gnn_be2': _L0_gnn_in['be2'], 'L0_ffn_W1': _L0_ffn_in['W1'], 'L0_ffn_b1': _L0_ffn_in['b1'], 'L0_ffn_Wg': _L0_ffn_in['Wg'], 'L0_ffn_bg': _L0_ffn_in['bg'], 'L0_ffn_Wd': _L0_ffn_in['Wd'], 'L0_ffn_bd': _L0_ffn_in['bd']}

def reference(x, src, dst, edge_weight, L0_gnn_eps, L0_gnn_W1, L0_gnn_b1, L0_gnn_g1, L0_gnn_be1, L0_gnn_W2, L0_gnn_b2, L0_gnn_g2, L0_gnn_be2, L0_ffn_W1, L0_ffn_b1, L0_ffn_Wg, L0_ffn_bg, L0_ffn_Wd, L0_ffn_bd):
    import jax
    import jax.numpy as jnp

    def _L0_gnn_ref(x, edge_row, edge_col, edge_vals, eps, W1, b1, g1, be1, W2, b2, g2, be2):
        import jax, jax.numpy as jnp
        import numpy as np
        N = 12500
        E = 400000
        DI = 256
        DO = 256
        BN_EPS = 1e-05

        def _bn_relu(h, gamma, beta):
            mean = jnp.mean(h, axis=0)
            var = jnp.var(h, axis=0)
            hn = (h - mean) * jax.lax.rsqrt(var + BN_EPS)
            return jax.nn.relu(hn * gamma + beta)
        n = x.shape[0]
        msgs = edge_vals[:, None] * x[edge_col]
        agg = jax.ops.segment_sum(msgs, edge_row, num_segments=n)
        h = (1.0 + eps[0]) * x + agg
        h = _bn_relu(h @ W1 + b1, g1, be1)
        h = _bn_relu(h @ W2 + b2, g2, be2)
        return h

    def _L0_ffn_ref(x, W1, b1, Wg, bg, Wd, bd):
        import jax, jax.numpy as jnp
        import numpy as np
        C = 256
        HID = 1024
        E = 8
        TEMP = 1.0
        orig_shape = x.shape
        xf = x.reshape(-1, orig_shape[-1])
        H = jax.nn.gelu(xf @ W1 + b1, approximate=False)
        probs = jax.nn.softmax((H @ Wg + bg) / TEMP, axis=-1)
        assign = jnp.argmax(probs, axis=-1)
        out = jnp.zeros_like(xf)
        for e in range(Wd.shape[0]):
            y = H @ Wd[e] + bd[e]
            sel = (assign == e)[:, None]
            out = out + jnp.where(sel, probs[:, e:e + 1] * y, 0.0)
        return out.reshape(orig_shape)
    x = x + _L0_gnn_ref(_layernorm(x, axis=-1), src, dst, edge_weight, L0_gnn_eps, L0_gnn_W1, L0_gnn_b1, L0_gnn_g1, L0_gnn_be1, L0_gnn_W2, L0_gnn_b2, L0_gnn_g2, L0_gnn_be2)
    x = x + _L0_ffn_ref(_layernorm(x, axis=-1)[None], L0_ffn_W1, L0_ffn_b1, L0_ffn_Wg, L0_ffn_bg, L0_ffn_Wd, L0_ffn_bd)[0]
    return x

_drawn_inputs = setup_inputs


def setup_inputs(seed=0):
    import zlib

    import numpy as np

    out = dict(_drawn_inputs(seed))
    spreads = {'L0_gnn_b1': (0.0, 0.8),
     'L0_gnn_g1': (1.0, 0.2),
     'L0_gnn_be1': (0.0, 0.1),
     'L0_gnn_b2': (0.0, 0.8),
     'L0_gnn_g2': (1.0, 0.2),
     'L0_gnn_be2': (0.0, 0.1),
     'L0_ffn_b1': (0.0, 0.706),
     'L0_ffn_bg': (0.0, 0.489),
     'L0_ffn_bd': (0.0, 0.692)}
    factors = {'L0_ffn_W1': 3.259, 'L0_ffn_Wg': 3.452, 'L0_ffn_Wd': 3.99}
    for name, (base, spread) in spreads.items():
        noise = np.random.default_rng([zlib.crc32(name.encode()), seed]).standard_normal(out[name].shape)
        drawn = base * np.exp(spread * noise) if base else spread * noise
        out[name] = jnp.asarray(drawn.astype(out[name].dtype))
    for name, factor in factors.items():
        out[name] = (out[name] * factor).astype(out[name].dtype)
    return out
```

```python
from contextlib import ExitStack

import concourse.bass as bass
from concourse import mybir

F32 = mybir.dt.float32
BF16 = mybir.dt.bfloat16
I32 = mybir.dt.int32
ALU = mybir.AluOpType
ACT = mybir.ActivationFunctionType
AX = mybir.AxisListType

P = 128
N = 12500
E = 200000
D = 256
DH = D // P
HID = 1024
KC = HID // P
NE = 8
EPS = 1e-5

CH = 4
CN = CH * P
NCH = -(-N // CN)
NPAD = NCH * CN
LAST = NCH - 1
DUMMY = NPAD
ROWS = NPAD + P
STREAMS = 4
ZRUNS = 16

G = 8
GE = G * P
ETILES = -(-E // P)
EB = -(-ETILES // P)
ECOLS = EB * P
EGROUPS = ECOLS // G
PAIRS = -(-ETILES // (2 * G))
GROUPS = 2 * PAIRS
FULL_BLOCKS = E // (P * P)
REST = E - FULL_BLOCKS * P * P
REST_ROWS = REST // P
REST_LAST = REST % P

BN_COLS = 500
BN_N = N // BN_COLS

CAP = -(-(N + 2 * (P - 1)) // 8) * 8
PAIRS_E = NE // 2
NOWHERE = PAIRS_E * CAP
STRAY = NOWHERE + P
REGION_ROWS = STRAY + CN
PAY_X = HID
PAY_PROB = HID + D
PAY_TOKEN = PAY_PROB + 1
PAY = PAY_PROB + 4
NO_TOKEN = 1 << 20
TTILES = N // P + NE


def ds(start, size):
    return bass.ds(start, size)


class Steps:

    def __init__(self, eng, sem):
        self.eng, self.sem, self.n = eng, sem, 0

    def restart(self):
        self.eng.sem_clear(self.sem)
        self.n = 0

    def link(self, ins):
        self.n += 1
        ins.then_inc(self.sem, 1)
        self.eng.wait_ge(self.sem, self.n)


class Memory:

    def __init__(self, nc, ctx, phase):
        self.nc, self.ctx, self.phase = nc, ctx, phase

    def sb(self, name, shape, dt=F32):
        return self.ctx.enter_context(self.nc.sbuf_tensor(f"{self.phase}_{name}", shape, dt))

    def ps(self, name, shape, dt=F32):
        return self.ctx.enter_context(self.nc.psum_tensor(f"{self.phase}_{name}", shape, dt))

    def sem(self, name):
        return self.ctx.enter_context(self.nc.semaphore(f"{self.phase}_{name}"))


def prepare(nc, c, x, src, dst, weight, gnn_eps, table, accs, halves, edge_cols, bases, flag):
    with ExitStack() as ctx:
        m = Memory(nc, ctx, "prep")
        xt = m.sb("xt", [P, 2, CH, D])
        xn = m.sb("xn", [P, 2, CH, D])
        own = m.sb("own", [P, 2, CH, D])
        stats = m.sb("stats", [P, CH, 6])
        mv = m.sb("mv", [P, 2, CH, 2])
        var = m.sb("var", [P, CH, 1])
        std = m.sb("std", [P, 2, CH, 1])
        rstd = m.sb("rstd", [P, CH, 1])
        eps1 = m.sb("eps1", [P, 1])
        eps_in = m.sb("eps_in", [P, 1])
        zeros = m.sb("zeros", [P, ROWS * D // P // ZRUNS])
        nsrc = m.sb("nsrc", [P, EB, P], I32)
        ndst = m.sb("ndst", [P, EB, P], I32)
        nw = m.sb("nw", [P, EB, P])
        nhalf = m.sb("nhalf", [P, EB, P], I32)
        nhi = m.sb("nhi", [P, EB, P], BF16)
        nlo = m.sb("nlo", [P, EB, P], BF16)
        nf = m.sb("nf", [P, EB, P])
        ng = m.sb("ng", [P, EB, P])
        dcol = m.sb("dcol", [P, ECOLS])
        bad = m.sb("bad", [P, EGROUPS, G])
        bad1 = m.sb("bad1", [P, 1])
        ramp = m.sb("ramp", [P, P], I32)
        line = m.sb("line", [P, P], I32)
        down = m.sb("down", [P, 1], I32)
        rev = m.sb("rev", [P, NE], I32)
        turned = m.ps("turned", [P, 2048])
        turned2 = m.ps("turned2", [P, 2048])

        x_in = [m.sem(f"x_in{s}") for s in range(2)]
        edge_in = m.sem("edge_in")
        eps_sem = m.sem("eps_in")
        zero_set = m.sem("zero_set")
        pads_set = m.sem("pads_set")
        slot_set = m.sem("slot_set")
        consts = m.sem("consts")
        iotas = m.sem("iotas")
        var_ready = m.sem("var_ready")
        std_ready = m.sem("std_ready")
        xn_ready = m.sem("xn_ready")
        own_ready = m.sem("own_ready")
        xn_out = [m.sem(f"xn_out{s}") for s in range(2)]
        own_out = [m.sem(f"own_out{s}") for s in range(2)]
        zero_out = m.sem("zero_out")
        half_ready = m.sem("half_ready")
        half_out = m.sem("half_out")
        flat_ready = m.sem("flat_ready")
        turned_ready = m.sem("turned_ready")
        turned_free = m.sem("turned_free")
        bad_ready = m.sem("bad_ready")
        flag_sum = m.sem("flag_sum")
        steps_sem = m.sem("steps")

        def chunk(t, i):
            return t[ds(i * CN, CN), :].rearrange("(j p) f -> p j f", p=P)

        def blocks(a):
            return a[0:FULL_BLOCKS * P * P].rearrange("(b q e) -> q b e", q=P, e=P)

        with nc.Block() as block:

            @block.sync
            def _(sp):
                sp.wait_ge(pads_set, 3)
                for to, a in ((nsrc, src), (ndst, dst), (nw, weight)):
                    sp.dma_start(to[:, 0:FULL_BLOCKS, :], blocks(a)).then_inc(edge_in, 16)
                    rest = a[FULL_BLOCKS * P * P:FULL_BLOCKS * P * P + REST_ROWS * P]
                    sp.dma_start(to[0:REST_ROWS, FULL_BLOCKS, :],
                                 rest.rearrange("(q e) -> q e", e=P)).then_inc(edge_in, 16)
                    if REST_LAST:
                        sp.dma_start(to[REST_ROWS:REST_ROWS + 1, FULL_BLOCKS, 0:REST_LAST],
                                     a[E - REST_LAST:E].rearrange("(q e) -> q e", q=1)).then_inc(edge_in, 16)

                def load(i, s):
                    sp.dma_start(xt[:, s, :, :], chunk(x, i)).then_inc(x_in[s], 16)

                load(0, 0)
                load(1, 1)
                with sp.Fori(1, LAST // 2, 1) as i:
                    for s in range(2):
                        sp.wait_ge(xn_ready, 2 * i + s - 1)
                        load(2 * i + s, s)
                sp.wait_ge(slot_set, 1)
                full = (N - LAST * CN) // P
                part = (N - LAST * CN) % P
                sp.dma_start(xt[:, 0, 0:full, :],
                             x[LAST * CN:LAST * CN + full * P, :].rearrange("(j p) f -> p j f", p=P)).then_inc(x_in[0], 16)
                sp.dma_start(xt[0:part, 0, full, :], x[N - part:N, :]).then_inc(x_in[0], 16)
                sp.wait_ge(zero_set, 1)
                for t in accs[1:]:
                    sp.dma_start(t.rearrange("(p r) f -> p (r f)", p=P).rearrange("p (z w) -> p z w", z=ZRUNS),
                                 zeros[:].unsqueeze(1).to_broadcast([P, ZRUNS, ROWS * D // P // ZRUNS])).then_inc(zero_out, 16)
                for t in (table, accs[0]):
                    sp.dma_start(t[NPAD:ROWS, :], zeros[:, 0:D]).then_inc(zero_out, 16)
                sp.wait_ge(half_ready, 2)
                for h, half in enumerate((nhi, nlo)):
                    sp.dma_start(halves[h:h + 1, :].rearrange("o (b q e) -> (o q) b e", q=P, e=P),
                                 half[:, :, :]).then_inc(half_out, 16)
                sp.wait_ge(zero_out, 16 * (STREAMS - 1 + 2))
                sp.wait_ge(half_out, 32)

            @block.gpsimd
            def _(pool):
                for t in (nsrc, ndst, nw):
                    pool.memset(t[:, FULL_BLOCKS:EB, :], 0).then_inc(pads_set, 1)
                pool.dma_start(eps_in[:], gnn_eps.partition_broadcast(P)).then_inc(eps_sem, 16)
                pool.memset(zeros[:], 0.0).then_inc(zero_set, 1)
                pool.iota(ramp[:], [[1, P]], base=0, channel_multiplier=-1).then_inc(iotas, 1)
                pool.iota(line[:], [[1, P]], base=0, channel_multiplier=0).then_inc(iotas, 1)
                pool.iota(down[:], [[0, 1]], base=0, channel_multiplier=1).then_inc(iotas, 1)
                pool.iota(rev[:], [[-1, NE]], base=NE, channel_multiplier=0).then_inc(iotas, 1)

            @block.scalar
            def _(act):
                act.wait_ge(consts, 1)

                def turn(i, s, before):
                    act.wait_ge(var_ready, i + 1)
                    act.activation(std[:, s], var[:], ACT.Sqrt).then_inc(std_ready, 1)
                    act.wait_ge(xn_ready, i + 1)
                    act.dma_start(chunk(table, i), xn[:, s]).then_inc(xn_out[s], 16)
                    if not isinstance(i, int) or i >= 2:
                        act.wait_ge(own_out[s], 16 * before)
                    act.activation(own[:, s], xn[:, s], ACT.Identity, scale=eps1[:, 0:1]).then_inc(own_ready, 1)
                    act.wait_ge(own_ready, i + 1)
                    act.dma_start(chunk(accs[0], i), own[:, s]).then_inc(own_out[s], 16)

                turn(0, 0, 0)
                turn(1, 1, 0)
                with act.Fori(1, LAST // 2, 1) as i:
                    turn(2 * i, 0, i)
                    turn(2 * i + 1, 1, i)
                turn(LAST, 0, LAST // 2)
                for s in range(2):
                    act.wait_ge(xn_out[s], 16 * (LAST // 2 + 1 - s))
                    act.wait_ge(own_out[s], 16 * (LAST // 2 + 1 - s))

            @block.vector
            def _(dve):
                steps = Steps(dve, steps_sem)
                dve.wait_ge(iotas, 4)
                dve.tensor_scalar(c.ident[:], ramp[:], 0.0, None, ALU.is_equal)
                dve.tensor_scalar(c.before[:], ramp[:], 0.0, None, ALU.is_lt)
                dve.tensor_scalar(c.after[:], ramp[:], 0.0, None, ALU.is_gt)
                dve.tensor_copy(c.line[:], line[:])
                dve.tensor_scalar(c.dummy[:], down[:], float(DUMMY), None, ALU.add)
                dve.tensor_copy(c.down[:], down[:])
                dve.tensor_copy(c.rev[:], rev[:])
                dve.memset(c.ones[:], 1.0)
                dve.memset(c.ones16[:], 1.0)
                dve.wait_ge(eps_sem, 16)
                dve.tensor_scalar(eps1[:], eps_in[:], 1.0, None, ALU.add).then_inc(consts, 1)
                dve.memset(c.joins[0:2, :], 1.0).then_inc(steps_sem, 1)
                dve.wait_ge(steps_sem, 1)
                dve.memset(c.joins[0:1, :], float(P)).then_inc(steps_sem, 1)
                dve.wait_ge(steps_sem, 2)

                dve.wait_ge(edge_in, 16 * 3 * (3 if REST_LAST else 2))
                steps.restart()
                steps.link(dve.tensor_scalar(nhalf[:], nsrc[:], 7, None, ALU.arith_shift_right))
                steps.link(dve.tensor_copy(nhi[:], nhalf[:]))
                dve.sem_inc(half_ready, 1)
                steps.link(dve.tensor_scalar(nhalf[:], nsrc[:], P - 1, None, ALU.bitwise_and))
                steps.link(dve.tensor_copy(nlo[:], nhalf[:]))
                dve.sem_inc(half_ready, 1)
                dve.tensor_copy(nf[:], nsrc[:]).then_inc(flat_ready, 1)
                dve.tensor_copy(ng[:], ndst[:]).then_inc(flat_ready, 1)

                def turn(i, s, before):
                    steps.restart()
                    dve.wait_ge(x_in[s], 16 * (before + 1) if not isinstance(i, int) or i < LAST else 16 * (before + 2))
                    for j in range(CH):
                        last = dve.bn_stats(stats[:, j, :], xt[:, s, j, :])
                    steps.link(last)
                    for j in range(CH):
                        last = dve.bn_aggr(mv[:, s, j, :], stats[:, j, :])
                    steps.link(last)
                    dve.tensor_scalar(var[:], mv[:, s, :, 1:2], EPS, None, ALU.add).then_inc(var_ready, 1)
                    dve.wait_ge(std_ready, i + 1)
                    steps.link(dve.reciprocal(rstd[:], std[:, s]))
                    if not isinstance(i, int) or i >= 2:
                        dve.wait_ge(xn_out[s], 16 * before)
                        dve.wait_ge(own_ready, i - 1)
                    for j in range(CH):
                        last = dve.tensor_scalar(xn[:, s, j, :], xt[:, s, j, :], mv[:, s, j, 0:1],
                                                 rstd[:, j, 0:1], ALU.subtract, ALU.mult)
                    last.then_inc(xn_ready, 1)

                turn(0, 0, 0)
                turn(1, 1, 0)
                with dve.Fori(1, LAST // 2, 1) as i:
                    turn(2 * i, 0, i)
                    turn(2 * i + 1, 1, i)
                dve.wait_ge(xn_ready, LAST)
                dve.memset(xt[:, 0], 0.0).then_inc(slot_set, 1)
                turn(LAST, 0, LAST // 2)

                dve.wait_ge(turned_ready, 1)
                dve.tensor_copy(edge_cols[:, :, 0, :], turned[:, 0:ECOLS].rearrange("p (g t) -> p g t", t=G)).then_inc(turned_free, 1)
                dve.wait_ge(turned_ready, 2)
                steps.restart()
                steps.link(dve.tensor_copy(dcol[:], turned2[:, 0:ECOLS]))
                dve.sem_inc(turned_free, 1)
                dve.wait_ge(turned_ready, 3)
                dve.tensor_copy(edge_cols[:, :, 2, :], turned[:, 0:ECOLS].rearrange("p (g t) -> p g t", t=G))
                dve.tensor_copy(edge_cols[:, :, 3, :], dcol[:].rearrange("p (g t) -> p g t", t=G))
                dve.wait_ge(turned_ready, 4)
                first = turned2[:, 0:EGROUPS]
                dve.tensor_copy(bases[0:1, :], turned2[0:1, 0:EGROUPS])
                steps.link(dve.tensor_tensor(edge_cols[:, :, 1, :], dcol[:].rearrange("p (g t) -> p g t", t=G),
                                             first.unsqueeze(2).to_broadcast([P, EGROUPS, G]), ALU.subtract))
                tile, row = divmod(E, P)
                if row:
                    dve.memset(edge_cols[row:P, tile // G, 1, tile % G:tile % G + 1], 0.0)
                    tile += 1
                if tile % G:
                    dve.memset(edge_cols[:, tile // G, 1, tile % G:G], 0.0)
                    tile += G - tile % G
                steps.link(dve.memset(edge_cols[:, tile // G:EGROUPS, 1, :], 0.0))
                local = edge_cols[:, :, 1, :]
                steps.link(dve.tensor_scalar(bad[:], local, float(P - 1), None, ALU.is_gt))
                steps.link(dve.scalar_tensor_tensor(bad[:], local, 0.0, bad[:], ALU.is_lt, ALU.add))
                dve.tensor_reduce(bad1[:], bad[:].rearrange("p g t -> p (g t)"), AX.X, ALU.add).then_inc(bad_ready, 1)
                dve.wait_ge(flag_sum, 1)
                steps.link(dve.tensor_scalar(bad1[:], turned[:, 0:1], 0.0, None, ALU.is_gt))
                steps.link(dve.tensor_copy(flag[:], bad1[:]))

            @block.tensor
            def _(pe):
                def turn(to, a):
                    for b in range(EB):
                        last = pe.transpose(to[:, b * P:(b + 1) * P], a[:, b, :], c.ident[:])
                    last.then_inc(turned_ready, 1)

                pe.wait_ge(flat_ready, 2)
                turn(turned, nf)
                turn(turned2, ng)
                pe.wait_ge(turned_free, 1)
                turn(turned, nw)
                pe.wait_ge(turned_free, 2)
                pe.matmul(turned2[:, 0:EGROUPS], c.ones[0:1, :],
                          dcol[0:1, :].rearrange("p (g t) -> p g t", t=G)[:, :, 0],
                          start=True, stop=True).then_inc(turned_ready, 1)
                pe.wait_ge(bad_ready, 1)
                pe.matmul(turned[:, 0:1], c.ones[:, :], bad1[:, :], start=True, stop=True).then_inc(flag_sum, 1)


def add_edges(nc, c, table, accs, halves, edge_cols, bases, flag):
    with ExitStack() as ctx:
        m = Memory(nc, ctx, "edge")
        rows = m.sb("rows", [2, 2, GE], BF16)
        window = m.sb("window", [P, 2, D])
        cols = m.sb("cols", [P, 2, 4, G])
        same = m.sb("same", [P, 2, G, P])
        pick = m.sb("pick", [P, 2, G, P])
        earlier = m.sb("earlier", [P, G, P])
        nearlier = m.sb("nearlier", [P, G])
        move = m.sb("move", [P, G])
        target = m.sb("target", [P, 2, G], I32)
        node = m.sb("node", [P, 2, G], I32)
        mix = m.sb("mix", [P, 2, G, P])
        gathered = m.sb("gathered", [P, 2, G, D])
        sums = m.sb("sums", [P, 2, G, D])
        ps_rows = m.ps("ps_rows", [P, G, P])
        ps_mix = m.ps("ps_mix", [P, G, P])
        ps_sums = m.ps("ps_sums", [P, G // 2, 2, D])

        rows_in = [m.sem(f"rows_in{s}") for s in range(2)]
        window_in = [m.sem(f"window_in{s}") for s in range(2)]
        rows_done = m.sem("rows_done")
        same_ready = m.sem("same_ready")
        pick_ready = m.sem("pick_ready")
        target_ready = m.sem("target_ready")
        mix_done = m.sem("mix_done")
        mix_ready = m.sem("mix_ready")
        sums_done = m.sem("sums_done")
        sums_ready = m.sem("sums_ready")
        added = [m.sem(f"added{k}") for k in range(STREAMS)]
        gather_in = m.sem("gather_in")
        pool_turn = m.sem("pool_turn")
        act_turn = m.sem("act_turn")
        sp_turn = m.sem("sp_turn")
        steps_sem = m.sem("steps")
        QUADS = G // 2
        PER = G // STREAMS

        def later(i, by):
            return not isinstance(i, int) or i >= by

        def all_pairs(eng, group):
            group(0, 0)
            group(1, 1)
            with eng.Fori(1, PAIRS, 1) as i:
                group(2 * i, 0)
                group(2 * i + 1, 1)

        with nc.Block() as block:

            @block.sync
            def _(sp):
                general = sp.value_load(flag[0:1, 0:1], min_val=0, max_val=1)

                def load_rows(i, s):
                    if later(i, 2):
                        sp.wait_ge(rows_done, i - 1)
                    sp.dma_start(rows[:, s, :], halves[:, ds(i * GE, GE)]).then_inc(rows_in[s], 16)

                def group(i, s, fast):
                    load_rows(i, s)
                    if fast:
                        if later(i, 2):
                            sp.wait_ge(sums_done, QUADS * (i - 1))
                            sp.sem_inc(sp_turn, 1)
                        base = sp.value_load(bases[0:1, ds(i, 1)], min_val=0, max_val=N - 1)
                        sp.dma_start(window[:, s, :], table[ds(base, P), :]).then_inc(window_in[s], 16)

                with sp.If(general):
                    all_pairs(sp, lambda i, s: group(i, s, False))
                    load_rows(GROUPS, 0)
                with sp.Else():
                    all_pairs(sp, lambda i, s: group(i, s, True))
                    load_rows(GROUPS, 0)
                sp.wait_ge(rows_in[0], 16 * (PAIRS + 1))

            @block.gpsimd
            def _(pool):
                general = pool.value_load(flag[0:1, 0:1], min_val=0, max_val=1)

                def gather(i, s):
                    pool.wait_ge(target_ready, i + 1)
                    if later(i, 2):
                        pool.wait_ge(sums_done, QUADS * (i - 1))
                    pool.sem_inc(pool_turn, 1)
                    for t in range(G):
                        pool.indirect_dma_start(
                            out=gathered[:, s, t, :], out_offset=None, in_=table[:, :],
                            in_offset=bass.IndirectOffsetOnAxis(ap=node[:, s, t:t + 1], axis=0),
                        ).then_inc(gather_in, 16)

                def group(i, s, fast):
                    if not fast:
                        gather(i, s)
                    for t in range(G):
                        if t == 0:
                            pool.wait_ge(target_ready, i + 1)
                        if t % 2 == 0:
                            pool.wait_ge(sums_ready, QUADS * i + t // 2 + 1)
                        if later(i, 1) or t >= STREAMS:
                            pool.wait_ge(added[t % STREAMS], 16 * (PER * i + t // STREAMS))
                        pool.sem_inc(pool_turn, 1)
                        pool.indirect_dma_start(
                            out=accs[t % STREAMS][:, :],
                            out_offset=bass.IndirectOffsetOnAxis(ap=target[:, s, t:t + 1], axis=0),
                            in_=sums[:, s, t, :], in_offset=None, compute_op=ALU.add,
                        ).then_inc(added[t % STREAMS], 16)

                with pool.If(general):
                    all_pairs(pool, lambda i, s: group(i, s, False))
                with pool.Else():
                    all_pairs(pool, lambda i, s: group(i, s, True))
                for k in range(STREAMS):
                    pool.wait_ge(added[k], 16 * PER * GROUPS)

            @block.vector
            def _(dve):
                general = dve.value_load(flag[0:1, 0:1], min_val=0, max_val=1)
                steps = Steps(dve, steps_sem)

                def group(i, s, fast):
                    steps.restart()
                    if later(i, 2):
                        dve.wait_ge(sums_done if not fast else mix_done, (QUADS if not fast else 1) * (i - 1))
                    steps.link(dve.tensor_copy(cols[:, s, :, :], edge_cols[:, ds(i, 1), :, :].rearrange("p o a t -> p (o a) t")))
                    target_f, local, wt, node_f = (cols[:, s, a, :] for a in range(4))
                    dve.wait_ge(rows_done, i + 1)
                    ins = dve.tensor_tensor(same[:, s], ps_rows[:, :, :],
                                            target_f.unsqueeze(2).to_broadcast([P, G, P]), ALU.is_equal)
                    ins.then_inc(same_ready, 1)
                    dve.wait_ge(same_ready, i + 1)
                    if fast:
                        for t in range(G):
                            ins = dve.tensor_scalar(pick[:, s, t, :], c.line[:], local[:, t:t + 1], wt[:, t:t + 1],
                                                    ALU.is_equal, ALU.mult)
                    else:
                        for t in range(G):
                            ins = dve.tensor_scalar(pick[:, s, t, :], same[:, s, t, :], wt[:, t:t + 1], None, ALU.mult)
                        dve.tensor_copy(node[:, s, :], node_f)
                    ins.then_inc(pick_ready, 1)
                    steps.link(dve.tensor_tensor(earlier[:], same[:, s],
                                                 c.before[:].unsqueeze(1).to_broadcast([P, G, P]), ALU.mult))
                    dve.tensor_reduce(nearlier[:], earlier[:], AX.X, ALU.add)
                    steps.link(dve.tensor_scalar(move[:], target_f, -1.0, c.dummy[:, 0:1], ALU.mult, ALU.add))
                    steps.link(dve.scalar_tensor_tensor(move[:], nearlier[:], 1.0, move[:], ALU.min, ALU.mult))
                    if later(i, 2):
                        for k in range(STREAMS):
                            dve.wait_ge(added[k], 16 * PER * (i - 1))
                    steps.link(dve.tensor_tensor(target[:, s, :], move[:], target_f, ALU.add))
                    dve.sem_inc(target_ready, 1)

                with dve.If(general):
                    all_pairs(dve, lambda i, s: group(i, s, False))
                with dve.Else():
                    all_pairs(dve, lambda i, s: group(i, s, True))

            @block.tensor
            def _(pe):
                general = pe.value_load(flag[0:1, 0:1], min_val=0, max_val=1)

                def weigh(i, s):
                    pe.wait_ge(pick_ready, i + 1)
                    if later(i, 1):
                        pe.wait_ge(mix_ready, i)
                    for t in range(G):
                        ins = pe.matmul(ps_mix[:, t, :], pick[:, s, t, :], same[:, s, t, :], start=True, stop=True)
                    ins.then_inc(mix_done, 1)

                def add_up(i, s, turns, fast):
                    if fast:
                        pe.wait_ge(mix_ready, i + 1)
                        pe.wait_ge(window_in[s], 16 * turns)
                    else:
                        pe.wait_ge(pick_ready, i + 1)
                        pe.wait_ge(gather_in, 16 * G * (i + 1))
                    for q in range(QUADS):
                        if later(i, 1):
                            pe.wait_ge(sums_ready, QUADS * (i - 1) + q + 1)
                        for u in range(2):
                            t = 2 * q + u
                            ins = pe.matmul(ps_sums[:, q, u, :], (mix if fast else pick)[:, s, t, :],
                                            window[:, s, :] if fast else gathered[:, s, t, :], start=True, stop=True)
                        ins.then_inc(sums_done, 1)

                def rows_of(i, s, turns):
                    pe.wait_ge(rows_in[s], 16 * turns)
                    if later(i, 1):
                        pe.wait_ge(same_ready, i)
                    for b in range(2):
                        ins = pe.matmul(ps_rows[:, b * (G // 2):(b + 1) * (G // 2), :], c.joins[:, :],
                                        rows[:, s, b * 512:(b + 1) * 512], start=True, stop=True)
                    ins.then_inc(rows_done, 1)

                def pair(p, fast):
                    for s in range(2):
                        i = 2 * p + s
                        rows_of(i + 1, 1 - s, p + 1 if s == 0 else p + 2)
                        if fast:
                            if later(i, 1):
                                add_up(i - 1, 1 - s, p if s == 0 else p + 1, fast)
                            weigh(i, s)
                        else:
                            add_up(i, s, p + 1, fast)

                def all_groups(fast):
                    rows_of(0, 0, 1)
                    pair(0, fast)
                    with pe.Fori(1, PAIRS, 1) as p:
                        pair(p, fast)
                    if fast:
                        add_up(GROUPS - 1, 1, PAIRS, fast)

                with pe.If(general):
                    all_groups(False)
                with pe.Else():
                    all_groups(True)

            @block.scalar
            def _(act):
                general = act.value_load(flag[0:1, 0:1], min_val=0, max_val=1)

                def group_mix(i, s):
                    act.wait_ge(mix_done, i + 1)
                    if later(i, 2):
                        act.wait_ge(sums_done, QUADS * (i - 1))
                    act.activation(mix[:, s], ps_mix[:, :, :], ACT.Copy).then_inc(mix_ready, 1)

                def group_sums(i, s):
                    for q in range(QUADS):
                        act.wait_ge(sums_done, QUADS * i + q + 1)
                        if later(i, 2) and q == 0:
                            for k in range(STREAMS):
                                act.wait_ge(added[k], 16 * PER * (i - 1))
                        act.activation(sums[:, s, 2 * q:2 * q + 2, :], ps_sums[:, q, :, :], ACT.Copy).then_inc(sums_ready, 1)

                with act.If(general):
                    all_pairs(act, group_sums)
                with act.Else():
                    group_mix(0, 0)
                    group_sums(0, 0)
                    group_mix(1, 1)
                    with act.Fori(1, PAIRS, 1) as p:
                        for s in range(2):
                            group_sums(2 * p + s - 1, 1 - s)
                            group_mix(2 * p + s, s)
                    group_sums(GROUPS - 1, 1)


class Constants:

    def __init__(self, m):
        self.ident = m.sb("ident", [P, P])
        self.before = m.sb("before", [P, P])
        self.after = m.sb("after", [P, P], BF16)
        self.line = m.sb("line", [P, P])
        self.down = m.sb("down", [P, 1])
        self.dummy = m.sb("dummy", [P, 1])
        self.rev = m.sb("rev", [P, NE])
        self.ones = m.sb("ones", [P, P])
        self.ones16 = m.sb("ones16", [P, P], BF16)
        self.joins = m.sb("joins", [2, P], BF16)


def linear(nc, c, accs, w1, b1, g1, be1, w2, b2, g2, be2, hid, scale, shift):
    with ExitStack() as ctx:
        m = Memory(nc, ctx, "lin")
        parts = m.sb("parts", [P, 2, STREAMS, CH, D])
        hT = m.sb("hT", [P, 2, DH, CN])
        w_sb = m.sb("w_sb", [P, 2, DH, D])
        vec = m.sb("vec", [P, 2, 3, DH])
        stats = m.sb("stats", [P, DH, BN_N, 6])
        mv = m.sb("mv", [P, DH, 2])
        std = m.sb("std", [P, DH])
        sc1 = m.sb("sc1", [P, DH])
        sh1 = m.sb("sh1", [P, DH])
        tmp = m.sb("tmp", [P, DH])
        ps_t = m.ps("ps_t", [P, 2, DH, CN])
        ps_h = m.ps("ps_h", [P, 2, DH, CN])

        params_in = m.sem("params_in")
        parts_in = [m.sem(f"parts_in{s}") for s in range(2)]
        sum_ready = m.sem("sum_ready")
        half_sum = m.sem("half_sum")
        turned = m.sem("turned")
        hT_ready = m.sem("hT_ready")
        hid_done = m.sem("hid_done")
        hid_ready = m.sem("hid_ready")
        var_ready = m.sem("var_ready")
        std_ready = m.sem("std_ready")
        norm_ready = m.sem("norm_ready")
        act_turn = m.sem("act_turn")
        dve_turn = m.sem("dve_turn")
        sp_turn = m.sem("sp_turn")
        steps_sem = m.sem("steps")

        def columns(i):
            return hid[:, :, ds(i * CN, CN)]

        def all_chunks(eng, chunk):
            chunk(0, 0, 0)
            chunk(1, 1, 0)
            with eng.Fori(1, LAST // 2, 1) as i:
                chunk(2 * i, 0, i)
                chunk(2 * i + 1, 1, i)
            chunk(LAST, 0, LAST // 2)

        def second(i):
            return not isinstance(i, int) or i >= 2

        with nc.Block() as block:

            @block.sync
            def _(sp):
                for a, (w, vs) in enumerate(((w1, (b1, g1, be1)), (w2, (b2, g2, be2)))):
                    sp.dma_start(w_sb[:, a, :, :], w.rearrange("(k p) o -> p k o", p=P)).then_inc(params_in, 16)
                    for b, v in enumerate(vs):
                        for h in range(DH):
                            sp.dma_start(vec[:, a, b, h:h + 1], v[h * P:(h + 1) * P].rearrange("(p o) -> p o", o=1)).then_inc(params_in, 16)

                def chunk(i, s, before):
                    if second(i):
                        sp.wait_ge(turned, i - 1)
                        sp.sem_inc(sp_turn, 1)
                    for k in range(STREAMS):
                        sp.dma_start(parts[:, s, k, :, :],
                                     accs[k][ds(i * CN, CN), :].rearrange("(j p) f -> p j f", p=P)).then_inc(parts_in[s], 16)

                all_chunks(sp, chunk)

            @block.gpsimd
            def _(pool):
                def chunk(i, s, before):
                    pool.wait_ge(parts_in[s], 16 * STREAMS * (before + 1))
                    pool.tensor_tensor(parts[:, s, 2], parts[:, s, 2], parts[:, s, 3], ALU.add).then_inc(half_sum, 1)

                all_chunks(pool, chunk)

            @block.vector
            def _(dve):
                steps = Steps(dve, steps_sem)

                def records(i, base):
                    dve.wait_ge(hid_ready, DH * (base + i + 1))
                    dve.sem_inc(dve_turn, 1)
                    for h in range(DH):
                        ins = dve.bn_stats(stats[:, h, ds(i, 1), :].rearrange("p o r -> p (o r)"), hid[:, h, ds(i * BN_COLS, BN_COLS)])
                    return ins

                def chunk1(i, s, before):
                    steps.restart()
                    dve.wait_ge(parts_in[s], 16 * STREAMS * (before + 1))
                    steps.link(dve.tensor_tensor(parts[:, s, 0], parts[:, s, 0], parts[:, s, 1], ALU.add))
                    dve.wait_ge(half_sum, i + 1)
                    ins = dve.tensor_tensor(parts[:, s, 0], parts[:, s, 0], parts[:, s, 2], ALU.add)
                    ins.then_inc(sum_ready, 1)
                    if not isinstance(i, int) or i >= 1:
                        records(i - 1, 0)

                def affine(a, sc, sh, base):
                    steps.restart()
                    steps.link(records(LAST, base))
                    for h in range(DH):
                        ins = dve.bn_aggr(mv[:, h, :], stats[:, h, :, :].rearrange("p c r -> p (c r)"))
                    steps.link(ins)
                    dve.tensor_scalar(tmp[:], mv[:, :, 1], EPS, None, ALU.add).then_inc(var_ready, 1)
                    dve.wait_ge(std_ready, a + 1)
                    steps.link(dve.reciprocal(tmp[:], std[:]))
                    steps.link(dve.tensor_tensor(sc[:], tmp[:], vec[:, a, 1, :], ALU.mult))
                    steps.link(dve.tensor_tensor(tmp[:], mv[:, :, 0], sc[:], ALU.mult))
                    steps.link(dve.tensor_tensor(sh[:], vec[:, a, 2, :], tmp[:], ALU.subtract))
                    dve.sem_inc(norm_ready, 1)

                dve.wait_ge(params_in, 16 * 2 * (1 + 3 * DH))
                all_chunks(dve, chunk1)
                affine(0, sc1, sh1, 0)
                dve.wait_ge(hid_ready, DH * NCH)
                with dve.Fori(0, LAST, 1) as i:
                    records(i, NCH)
                affine(1, scale, shift, NCH)

            @block.tensor
            def _(pe):
                pe.wait_ge(params_in, 16 * 2 * (1 + 3 * DH))

                def turn(i, s):
                    pe.wait_ge(sum_ready, i + 1)
                    if second(i):
                        pe.wait_ge(hT_ready, i - 1)
                    for h in range(DH):
                        for j in range(CH):
                            ins = pe.transpose(ps_t[:, s, h, j * P:(j + 1) * P], parts[:, s, 0, j, h * P:(h + 1) * P], c.ident[:])
                    ins.then_inc(turned, 1)

                def layer(i, s, a, base):
                    pe.wait_ge(hT_ready, base + i + 1)
                    if base or second(i):
                        pe.wait_ge(hid_ready, DH * (base + i - 1))
                    for o in range(DH):
                        for k in range(DH):
                            ins = pe.matmul(ps_h[:, s, o, :], w_sb[:, a, k, o * P:(o + 1) * P], hT[:, s, k, :],
                                            start=(k == 0), stop=(k == DH - 1))
                        ins.then_inc(hid_done, 1)

                turn(0, 0)
                turn(1, 1)
                layer(0, 0, 0, 0)
                with pe.Fori(1, LAST // 2, 1) as i:
                    turn(2 * i, 0)
                    layer(2 * i - 1, 1, 0, 0)
                    turn(2 * i + 1, 1)
                    layer(2 * i, 0, 0, 0)
                turn(LAST, 0)
                layer(LAST - 1, 1, 0, 0)
                layer(LAST, 0, 0, 0)
                with pe.Fori(0, LAST // 2, 1) as i:
                    layer(2 * i, 1, 1, NCH)
                    layer(2 * i + 1, 0, 1, NCH)
                layer(LAST, 1, 1, NCH)

            @block.scalar
            def _(act):
                act.wait_ge(params_in, 16 * 2 * (1 + 3 * DH))

                def keep_turned(i, s):
                    act.wait_ge(turned, i + 1)
                    if second(i):
                        act.wait_ge(hid_done, DH * (i - 1))
                    act.activation(hT[:, s], ps_t[:, s], ACT.Copy).then_inc(hT_ready, 1)

                def keep_hidden(i, s, a, base):
                    for o in range(DH):
                        act.wait_ge(hid_done, DH * (base + i) + o + 1)
                        act.sem_inc(act_turn, 1)
                        act.activation(hid[:, o, ds(i * CN, CN)], ps_h[:, s, o, :], ACT.Identity,
                                       bias=vec[:, a, 0, o:o + 1]).then_inc(hid_ready, 1)

                def norm(i, s):
                    act.wait_ge(hid_done, DH * (NCH + i - 1))
                    act.sem_inc(act_turn, 1)
                    for k in range(DH):
                        ins = act.activation(hT[:, s, k, :], hid[:, k, ds(i * CN, CN)], ACT.Relu,
                                             scale=sc1[:, k:k + 1], bias=sh1[:, k:k + 1])
                    ins.then_inc(hT_ready, 1)

                keep_turned(0, 0)
                keep_turned(1, 1)
                keep_hidden(0, 0, 0, 0)
                with act.Fori(1, LAST // 2, 1) as i:
                    keep_turned(2 * i, 0)
                    keep_hidden(2 * i - 1, 1, 0, 0)
                    keep_turned(2 * i + 1, 1)
                    keep_hidden(2 * i, 0, 0, 0)
                keep_turned(LAST, 0)
                keep_hidden(LAST - 1, 1, 0, 0)
                keep_hidden(LAST, 0, 0, 0)
                act.wait_ge(var_ready, 1)
                act.activation(std[:], tmp[:], ACT.Sqrt).then_inc(std_ready, 1)
                act.wait_ge(norm_ready, 1)
                norm(0, 1)
                with act.Fori(0, LAST // 2, 1) as i:
                    norm(2 * i + 1, 0)
                    keep_hidden(2 * i, 1, 1, NCH)
                    norm(2 * i + 2, 1)
                    keep_hidden(2 * i + 1, 0, 1, NCH)
                keep_hidden(LAST, 1, 1, NCH)
                act.wait_ge(var_ready, 2)
                act.activation(std[:], tmp[:], ACT.Sqrt).then_inc(std_ready, 1)


def gate(nc, c, x, w1, b1, wg, bg, hid, scale, shift, regions, ends):
    with ExitStack() as ctx:
        m = Memory(nc, ctx, "gate")
        w_sb = m.sb("w_sb", [P, DH, HID])
        wg_sb = m.sb("wg_sb", [P, KC, NE])
        b_sb = m.sb("b_sb", [P, KC])
        bg_sb = m.sb("bg_sb", [P, NE])
        out2 = m.sb("out2", [P, DH, CN])
        xt = m.sb("xt", [P, CH, D])
        xn = m.sb("xn", [P, CH, D])
        xnT = m.sb("xnT", [P, DH, CN])
        act_h = m.sb("act_h", [P, KC, CN])
        pay = m.sb("pay", [P, CH, PAY])
        stats = m.sb("stats", [P, CH, 6])
        mv = m.sb("mv", [P, CH, 2])
        var = m.sb("var", [P, CH, 1])
        std = m.sb("std", [P, CH, 1])
        rstd = m.sb("rstd", [P, CH, 1])
        logit = m.sb("logit", [P, CH, NE])
        best = m.sb("best", [P, CH])
        expd = m.sb("expd", [P, CH, NE])
        total = m.sb("total", [P, CH])
        key = m.sb("key", [P, CH, NE])
        chosen = m.sb("chosen", [P, CH, NE])
        chosen16 = m.sb("chosen16", [P, CH, NE], BF16)
        token = m.sb("token", [P, CH])
        token_i = m.sb("token_i", [P, CH], I32)
        real = m.sb("real", [P, CH])
        stray = m.sb("stray", [P, CH])
        first = m.sb("first", [P, NE])
        first_i = m.sb("first_i", [P, NE], I32)
        sign_i = m.sb("sign_i", [P, NE], I32)
        sign = m.sb("sign", [P, NE])
        place = m.sb("place", [P, CH, NE])
        where = m.sb("where", [P, CH])
        where_i = m.sb("where_i", [P, CH], I32)
        ps_x = m.ps("ps_x", [P, CH, D])
        ps_h = m.ps("ps_h", [P, 2, CN])
        ps_b = m.ps("ps_b", [P, 2, CH, P])
        ps_g = m.ps("ps_g", [P, CH, NE])
        ps_p = m.ps("ps_p", [P, CH + 1, NE])

        params_in = m.sem("params_in")
        iotas = m.sem("iotas")
        consts = m.sem("consts")
        x_in = m.sem("x_in")
        out2_ready = m.sem("out2_ready")
        turned_back = m.sem("turned_back")
        var_ready = m.sem("var_ready")
        std_ready = m.sem("std_ready")
        xn_ready = m.sem("xn_ready")
        xn_turned = m.sem("xn_turned")
        xnT_ready = m.sem("xnT_ready")
        h_done = m.sem("h_done")
        h_ready = m.sem("h_ready")
        back_done = m.sem("back_done")
        back_ready = m.sem("back_ready")
        logit_done = m.sem("logit_done")
        logit_ready = m.sem("logit_ready")
        exp_ready = m.sem("exp_ready")
        chosen_ready = m.sem("chosen_ready")
        place_done = m.sem("place_done")
        pay_ready = m.sem("pay_ready")
        sent = m.sem("sent")
        act_turn = m.sem("act_turn")
        pool_turn = m.sem("pool_turn")
        steps_sem = m.sem("steps")
        PARAMS = 3 + KC

        def all_chunks(eng, chunk):
            chunk(0)
            with eng.Fori(1, LAST, 1) as i:
                chunk(i)
            chunk(LAST)

        def later(i):
            return not isinstance(i, int) or i >= 1

        with nc.Block() as block:

            @block.sync
            def _(sp):
                sp.dma_start(w_sb[:], w1.rearrange("(k p) o -> p k o", p=P)).then_inc(params_in, 16)
                sp.dma_start(wg_sb[:], wg.rearrange("(k p) o -> p k o", p=P)).then_inc(params_in, 16)
                sp.dma_start(bg_sb[:], bg.partition_broadcast(P)).then_inc(params_in, 16)
                for k in range(KC):
                    sp.dma_start(b_sb[:, k:k + 1], b1[k * P:(k + 1) * P].rearrange("(p o) -> p o", o=1)).then_inc(params_in, 16)

                def chunk(i):
                    if later(i):
                        sp.wait_ge(var_ready, i)
                    if isinstance(i, int) and i == LAST:
                        full, part = divmod(N - LAST * CN, P)
                        sp.dma_start(xt[:, 0:full, :],
                                     x[LAST * CN:LAST * CN + full * P, :].rearrange("(j p) f -> p j f", p=P)).then_inc(x_in, 16)
                        sp.dma_start(xt[0:part, full, :], x[N - part:N, :]).then_inc(x_in, 16)
                    else:
                        sp.dma_start(xt[:], x[ds(i * CN, CN), :].rearrange("(j p) f -> p j f", p=P)).then_inc(x_in, 16)

                all_chunks(sp, chunk)

            @block.gpsimd
            def _(pool):
                pool.iota(token_i[:], [[P, CH]], base=0, channel_multiplier=1).then_inc(iotas, 1)
                pool.iota(first_i[:], [[CAP, PAIRS_E], [CAP - 1, 2]], base=0, channel_multiplier=0).then_inc(iotas, 1)
                pool.iota(sign_i[:], [[0, PAIRS_E], [-2, 2]], base=1, channel_multiplier=0).then_inc(iotas, 1)

                def chunk(i):
                    pool.wait_ge(pay_ready, i + 1)
                    pool.wait_ge(back_ready, KC * (i + 1))
                    pool.sem_inc(pool_turn, 1)
                    for j in range(CH):
                        pool.indirect_dma_start(
                            out=regions[:, :],
                            out_offset=bass.IndirectOffsetOnAxis(ap=where_i[:, j:j + 1], axis=0),
                            in_=pay[:, j, :], in_offset=None,
                        ).then_inc(sent, 16)

                all_chunks(pool, chunk)
                pool.wait_ge(sent, 16 * CH * NCH)

            @block.scalar
            def _(act):
                act.wait_ge(params_in, 16 * PARAMS)
                act.wait_ge(consts, 1)

                def chunk(i):
                    if later(i):
                        act.wait_ge(turned_back, i)
                    act.sem_inc(act_turn, 1)
                    for k in range(DH):
                        ins = act.activation(out2[:, k, :], hid[:, k, ds(i * CN, CN)], ACT.Relu,
                                             scale=scale[:, k:k + 1], bias=shift[:, k:k + 1])
                    ins.then_inc(out2_ready, 1)
                    act.wait_ge(var_ready, i + 1)
                    act.activation(std[:], var[:], ACT.Sqrt).then_inc(std_ready, 1)
                    act.wait_ge(xn_turned, i + 1)
                    act.activation(xnT[:], ps_x[:].rearrange("p c f -> p (c f)").rearrange("p (k n) -> p k n", k=DH), ACT.Copy).then_inc(xnT_ready, 1)
                    for k in range(KC):
                        act.wait_ge(h_done, KC * i + k + 1)
                        if k == 0 and later(i):
                            act.wait_ge(logit_done, i)
                            act.wait_ge(back_done, KC * i)
                        act.activation(act_h[:, k, :], ps_h[:, k % 2, :], ACT.Gelu, bias=b_sb[:, k:k + 1]).then_inc(h_ready, 1)
                    act.wait_ge(logit_ready, i + 1)
                    act.activation(expd[:], logit[:], ACT.Exp).then_inc(exp_ready, 1)

                all_chunks(act, chunk)

            @block.vector
            def _(dve):
                steps = Steps(dve, steps_sem)
                dve.memset(pay[:, :, PAY_TOKEN:PAY], 0.0)
                dve.wait_ge(iotas, 3)
                steps.link(dve.tensor_copy(sign[:], sign_i[:]))
                steps.link(dve.tensor_copy(token[:], token_i[:]))
                steps.link(dve.tensor_scalar(stray[:], token[:], float(STRAY), None, ALU.add))
                steps.link(dve.tensor_copy(first[:], first_i[:]))
                dve.wait_ge(params_in, 16 * PARAMS)
                dve.sem_inc(consts, 1)

                def chunk(i):
                    steps.restart()
                    if isinstance(i, int) and i == LAST:
                        dve.wait_ge(x_in, 16 * (LAST + 2))
                    else:
                        dve.wait_ge(x_in, 16 * (i + 1))
                    dve.wait_ge(turned_back, i + 1)
                    if later(i):
                        dve.wait_ge(sent, 16 * CH * i)
                    steps.link(dve.tensor_tensor(pay[:, :, PAY_X:PAY_X + D], xt[:], ps_x[:], ALU.add))
                    for j in range(CH):
                        ins = dve.bn_stats(stats[:, j, :], pay[:, j, PAY_X:PAY_X + D])
                    steps.link(ins)
                    for j in range(CH):
                        ins = dve.bn_aggr(mv[:, j, :], stats[:, j, :])
                    steps.link(ins)
                    dve.tensor_scalar(var[:], mv[:, :, 1:2], EPS, None, ALU.add).then_inc(var_ready, 1)
                    dve.wait_ge(std_ready, i + 1)
                    steps.link(dve.reciprocal(rstd[:], std[:]))
                    for j in range(CH):
                        ins = dve.tensor_scalar(xn[:, j, :], pay[:, j, PAY_X:PAY_X + D], mv[:, j, 0:1],
                                                rstd[:, j, 0:1], ALU.subtract, ALU.mult)
                    ins.then_inc(xn_ready, 1)
                    for k in range(KC):
                        dve.wait_ge(back_done, KC * i + k + 1)
                        dve.tensor_copy(pay[:, :, k * P:(k + 1) * P], ps_b[:, k % 2, :, :]).then_inc(back_ready, 1)
                    dve.wait_ge(logit_done, i + 1)
                    wide = [P, CH, NE]
                    steps.link(dve.tensor_tensor(logit[:], ps_g[:], bg_sb[:].unsqueeze(1).to_broadcast(wide), ALU.add))
                    steps.link(dve.tensor_reduce(best[:], logit[:], AX.X, ALU.max))
                    steps.link(dve.tensor_tensor(logit[:], logit[:], best[:].unsqueeze(2).to_broadcast(wide), ALU.subtract))
                    dve.sem_inc(logit_ready, 1)
                    steps.link(dve.tensor_scalar(key[:], logit[:], 0.0, None, ALU.is_ge))
                    steps.link(dve.tensor_tensor(key[:], key[:], c.rev[:].unsqueeze(1).to_broadcast(wide), ALU.mult))
                    steps.link(dve.tensor_reduce(best[:], key[:], AX.X, ALU.max))
                    dve.tensor_tensor(chosen[:], key[:], best[:].unsqueeze(2).to_broadcast(wide), ALU.is_equal)
                    steps.link(dve.tensor_scalar(real[:], token[:], float(N), None, ALU.is_lt))
                    steps.link(dve.tensor_tensor(chosen[:], chosen[:], real[:].unsqueeze(2).to_broadcast(wide), ALU.mult))
                    dve.tensor_tensor(chosen16[:], chosen[:], sign[:].unsqueeze(1).to_broadcast(wide), ALU.mult).then_inc(chosen_ready, 1)
                    dve.wait_ge(exp_ready, i + 1)
                    steps.link(dve.tensor_reduce(total[:], expd[:], AX.X, ALU.add))
                    dve.reciprocal(pay[:, :, PAY_PROB], total[:])
                    dve.tensor_copy(pay[:, :, PAY_TOKEN], token[:])
                    dve.wait_ge(place_done, i + 1)
                    steps.link(dve.tensor_tensor(place[:], ps_p[:, 0:CH, :], first[:].unsqueeze(1).to_broadcast(wide), ALU.add))
                    steps.link(dve.tensor_tensor(place[:], place[:], chosen[:], ALU.mult))
                    steps.link(dve.tensor_reduce(where[:], place[:], AX.X, ALU.add))
                    steps.link(dve.tensor_scalar(real[:], real[:], -1.0, 1.0, ALU.mult, ALU.add))
                    steps.link(dve.tensor_tensor(real[:], real[:], stray[:], ALU.mult))
                    steps.link(dve.tensor_tensor(where_i[:], where[:], real[:], ALU.add))
                    dve.sem_inc(pay_ready, 1)
                    dve.tensor_tensor(first[:], first[:], ps_p[:, CH, :], ALU.add)
                    steps.link(dve.tensor_scalar(token[:], token[:], float(CN), None, ALU.add))

                all_chunks(dve, chunk)
                steps.restart()
                steps.link(dve.tensor_scalar(sign[:], sign[:], 0.5 * (P - 1), -0.5 * (P - 1), ALU.mult, ALU.add))
                steps.link(dve.tensor_tensor(ends[:], first[:], sign[:], ALU.add))

            @block.tensor
            def _(pe):
                pe.wait_ge(params_in, 16 * PARAMS)

                def chunk(i):
                    pe.wait_ge(out2_ready, i + 1)
                    if later(i):
                        pe.wait_ge(xnT_ready, i)
                    for j in range(CH):
                        for k in range(DH):
                            ins = pe.transpose(ps_x[:, j, k * P:(k + 1) * P], out2[:, k, j * P:(j + 1) * P], c.ident[:])
                    ins.then_inc(turned_back, 1)
                    pe.wait_ge(xn_ready, i + 1)
                    flat = ps_x[:].rearrange("p c f -> p (c f)")
                    for k in range(DH):
                        for j in range(CH):
                            ins = pe.transpose(flat[:, k * CN + j * P:k * CN + (j + 1) * P], xn[:, j, k * P:(k + 1) * P], c.ident[:])
                    ins.then_inc(xn_turned, 1)
                    pe.wait_ge(xnT_ready, i + 1)

                    def back(k):
                        pe.wait_ge(h_ready, KC * i + k + 1)
                        if k >= 2 or later(i):
                            pe.wait_ge(back_ready, KC * i + k - 1)
                        for j in range(CH):
                            ins = pe.transpose(ps_b[:, k % 2, j, :], act_h[:, k, j * P:(j + 1) * P], c.ident[:])
                        ins.then_inc(back_done, 1)

                    for k in range(KC):
                        if k >= 2 or later(i):
                            pe.wait_ge(h_ready, KC * i + k - 1)
                        for q in range(DH):
                            ins = pe.matmul(ps_h[:, k % 2, :], w_sb[:, q, k * P:(k + 1) * P], xnT[:, q, :],
                                            start=(q == 0), stop=(q == DH - 1))
                        ins.then_inc(h_done, 1)
                        if k >= 1:
                            back(k - 1)
                    back(KC - 1)
                    if later(i):
                        pe.wait_ge(logit_ready, i)
                    for j in range(CH):
                        for k in range(KC):
                            ins = pe.matmul(ps_g[:, j, :], act_h[:, k, j * P:(j + 1) * P], wg_sb[:, k, :],
                                            start=(k == 0), stop=(k == KC - 1))
                    ins.then_inc(logit_done, 1)
                    pe.wait_ge(chosen_ready, i + 1)
                    if later(i):
                        pe.wait_ge(pay_ready, i)
                    for j in range(CH + 1):
                        for b in range(min(j, CH)):
                            ins = pe.matmul(ps_p[:, j, :], c.ones16[:], chosen16[:, b, :],
                                            start=(b == 0), stop=(j == CH and b == CH - 1))
                        if j < CH:
                            ins = pe.matmul(ps_p[:, j, :], c.after[:], chosen16[:, j, :], start=(j == 0), stop=True)
                    ins.then_inc(place_done, 1)

                all_chunks(pe, chunk)


def experts(nc, c, wd, bd, regions, ends, out):
    with ExitStack() as ctx:
        m = Memory(nc, ctx, "exp")
        w_sb = m.sb("w_sb", [P, NE, KC, D])
        b_sb = m.sb("b_sb", [P, NE, D])
        none = m.sb("none", [P, PAY])
        tile_i = m.sb("tile_i", [P, TTILES], I32)
        tile_f = m.sb("tile_f", [P, TTILES])
        past = m.sb("past", [P, TTILES])
        row = m.sb("row", [P, TTILES])
        expert = m.sb("expert", [P, TTILES])
        row_i = m.sb("row_i", [P, TTILES], I32)
        expert_i = m.sb("expert_i", [P, TTILES], I32)
        first = m.sb("first", [P, NE], I32)
        ntiles = m.sb("ntiles", [P, NE], I32)
        ntiles_f = m.sb("ntiles_f", [P, NE])
        cum = m.sb("cum", [P, NE])
        sign_i = m.sb("sign_i", [P, NE], I32)
        sign = m.sb("sign", [P, NE])
        offset = m.sb("offset", [P, NE])
        pay = m.sb("pay", [P, 3, PAY])
        hT = m.sb("hT", [P, 2, KC, P])
        res = m.sb("res", [P, 2, D])
        token = m.sb("token", [P, 2, 1], I32)
        ps_t = m.ps("ps_t", [P, 2, KC, P])
        ps_y = m.ps("ps_y", [P, 2, 512])

        w_in = m.sem("w_in")
        iotas = m.sem("iotas")
        none_set = m.sem("none_set")
        none_out = m.sem("none_out")
        table_ready = m.sem("table_ready")
        pay_in = [m.sem(f"pay_in{s}") for s in range(3)]
        turned = m.sem("turned")
        hT_ready = m.sem("hT_ready")
        y_done = m.sem("y_done")
        res_ready = m.sem("res_ready")
        out_done = [m.sem(f"out_done{s}") for s in range(2)]
        pool_turn = m.sem("pool_turn")
        dve_turn = m.sem("dve_turn")
        sp_turn = m.sem("sp_turn")
        steps_sem = m.sem("steps")
        U = 6
        TURNS = -(-TTILES // U)
        FULL = TTILES // U

        def all_tiles(eng, tile):
            for u in range(U):
                tile(u, u, 0)
            with eng.Fori(1, FULL, 1) as i:
                for u in range(U):
                    tile(U * i + u, u, i)
            for u in range(TTILES - U * FULL):
                tile(U * FULL + u, u, FULL)

        def later(i, by):
            return not isinstance(i, int) or i >= by

        with nc.Block() as block:

            @block.sync
            def _(sp):
                sp.wait_ge(none_set, 1)
                for e in range(NE):
                    end = sp.value_load(ends[0:1, e:e + 1], min_val=0, max_val=NOWHERE - P)
                    sp.dma_start(regions[ds(end, P), :], none[:]).then_inc(none_out, 16)
                sp.dma_start(regions[NOWHERE:NOWHERE + P, :], none[:]).then_inc(none_out, 16)
                sp.dma_start(b_sb[:].rearrange("p e f -> p (e f)"), bd.rearrange("e f -> (e f)").partition_broadcast(P)).then_inc(w_in, 16)
                for e in range(NE):
                    sp.dma_start(w_sb[:, e, :, :], wd[e].rearrange("(k p) o -> p k o", p=P)).then_inc(w_in, 16)
                sp.wait_ge(none_out, 16 * (NE + 1))
                sp.wait_ge(table_ready, 1)

                def tile(i, u, turn):
                    if later(i, 3):
                        sp.wait_ge(res_ready, i - 2)
                        sp.sem_inc(sp_turn, 1)
                    at = sp.value_load(row_i[0:1, ds(i, 1)], min_val=0, max_val=NOWHERE)
                    sp.dma_start(pay[:, u % 3, :], regions[ds(at, P), :]).then_inc(pay_in[u % 3], 16)

                all_tiles(sp, tile)

            @block.gpsimd
            def _(pool):
                pool.iota(tile_i[:], [[1, TTILES]], base=0, channel_multiplier=0).then_inc(iotas, 1)
                pool.iota(first[:], [[CAP, PAIRS_E], [CAP - P, 2]], base=0, channel_multiplier=0).then_inc(iotas, 1)
                pool.iota(sign_i[:], [[0, PAIRS_E], [-2, 2]], base=1, channel_multiplier=0).then_inc(iotas, 1)

                def tile(i, u, turn):
                    pool.wait_ge(res_ready, i + 1)
                    pool.sem_inc(pool_turn, 1)
                    pool.indirect_dma_start(
                        out=out[:, :], out_offset=bass.IndirectOffsetOnAxis(ap=token[:, u % 2, :], axis=0),
                        in_=res[:, u % 2, :], in_offset=None, bounds_check=N - 1, oob_is_err=False,
                    ).then_inc(out_done[u % 2], 16)

                all_tiles(pool, tile)
                pool.wait_ge(out_done[0], 16 * ((TTILES + 1) // 2))
                pool.wait_ge(out_done[1], 16 * (TTILES // 2))

            @block.scalar
            def _(act):
                def tile(i, u, turn):
                    s = u % 2
                    act.wait_ge(turned, i + 1)
                    if later(i, 2):
                        act.wait_ge(y_done, i - 1)
                    act.activation(hT[:, s], ps_t[:, s], ACT.Copy).then_inc(hT_ready, 1)

                all_tiles(act, tile)

            @block.vector
            def _(dve):
                steps = Steps(dve, steps_sem)
                steps.link(dve.memset(none[:], 0.0))
                dve.memset(none[:, PAY_TOKEN:PAY_TOKEN + 1], float(NO_TOKEN)).then_inc(none_set, 1)
                dve.wait_ge(iotas, 3)
                steps.link(dve.tensor_copy(sign[:], sign_i[:]))
                steps.link(dve.tensor_copy(tile_f[:], tile_i[:]))
                steps.link(dve.tensor_tensor(cum[:], ends[:], first[:], ALU.subtract))
                steps.link(dve.tensor_tensor(cum[:], cum[:], sign[:], ALU.mult))
                steps.link(dve.tensor_scalar(cum[:], cum[:], float(P - 1), None, ALU.add))
                steps.link(dve.tensor_copy(ntiles[:], cum[:]))
                steps.link(dve.tensor_scalar(ntiles[:], ntiles[:], 7, None, ALU.arith_shift_right))
                steps.link(dve.tensor_copy(ntiles_f[:], ntiles[:]))
                steps.link(dve.tensor_copy(cum[:], ntiles_f[:]))
                for e in range(1, NE):
                    steps.link(dve.tensor_tensor(cum[:, e:e + 1], cum[:, e:e + 1], cum[:, e - 1:e], ALU.add))
                steps.link(dve.tensor_tensor(offset[:], ntiles_f[:], cum[:], ALU.subtract))
                steps.link(dve.tensor_tensor(offset[:], offset[:], sign[:], ALU.mult))
                steps.link(dve.scalar_tensor_tensor(offset[:], offset[:], float(P), first[:], ALU.mult, ALU.add))
                steps.link(dve.memset(expert[:], 0.0))
                for e in range(NE):
                    steps.link(dve.scalar_tensor_tensor(expert[:], tile_f[:], cum[:, e:e + 1], expert[:], ALU.is_ge, ALU.add))
                steps.link(dve.tensor_scalar(row[:], expert[:], float(NE), float(NOWHERE), ALU.is_equal, ALU.mult))
                for e in range(NE):
                    way = float(P) if e % 2 == 0 else float(-P)
                    steps.link(dve.tensor_scalar(past[:], tile_f[:], way, offset[:, e:e + 1], ALU.mult, ALU.add))
                    steps.link(dve.scalar_tensor_tensor(past[:], expert[:], float(e), past[:], ALU.is_equal, ALU.mult))
                    steps.link(dve.tensor_tensor(row[:], row[:], past[:], ALU.add))
                steps.link(dve.tensor_copy(row_i[:], row[:]))
                steps.link(dve.tensor_scalar(expert_i[:], expert[:], float(NE - 1), None, ALU.min))
                dve.sem_inc(table_ready, 1)
                dve.wait_ge(w_in, 16 * (NE + 1))
                dve.sem_inc(dve_turn, 1)

                def tile(i, u, turn):
                    s = u % 2
                    steps.restart()
                    e = dve.value_load(expert_i[0:1, ds(i, 1)], min_val=0, max_val=NE - 1)
                    dve.wait_ge(y_done, i + 1)
                    if later(i, 2):
                        dve.wait_ge(out_done[s], 16 * (3 * turn + u // 2))
                    dve.sem_inc(dve_turn, 1)
                    steps.link(dve.tensor_tensor(res[:, s, :], ps_y[:, s, 0:D], b_sb[:, ds(e, 1), :].rearrange("p o f -> p (o f)"), ALU.add))
                    dve.tensor_copy(token[:, s, :], pay[:, u % 3, PAY_TOKEN:PAY_TOKEN + 1])
                    dve.scalar_tensor_tensor(res[:, s, :], res[:, s, :], pay[:, u % 3, PAY_PROB:PAY_PROB + 1],
                                             pay[:, u % 3, PAY_X:PAY_X + D], ALU.mult, ALU.add).then_inc(res_ready, 1)

                all_tiles(dve, tile)

            @block.tensor
            def _(pe):
                pe.wait_ge(table_ready, 1)
                pe.wait_ge(w_in, 16 * (NE + 1))

                def turn_tile(i, u, turn):
                    s = u % 2
                    pe.wait_ge(pay_in[u % 3], 16 * (2 * turn + u // 3 + 1))
                    if later(i, 2):
                        pe.wait_ge(hT_ready, i - 1)
                    for k in range(KC):
                        ins = pe.transpose(ps_t[:, s, k, :], pay[:, u % 3, k * P:(k + 1) * P], c.ident[:])
                    ins.then_inc(turned, 1)

                def multiply(i, s):
                    e = pe.value_load(expert_i[0:1, ds(i, 1)], min_val=0, max_val=NE - 1)
                    pe.wait_ge(hT_ready, i + 1)
                    if later(i, 2):
                        pe.wait_ge(res_ready, i - 1)
                    for k in range(KC):
                        ins = pe.matmul(ps_y[:, s, 0:D], hT[:, s, k, :], w_sb[:, ds(e, 1), k, :].rearrange("p o f -> p (o f)"),
                                        start=(k == 0), stop=(k == KC - 1))
                    ins.then_inc(y_done, 1)

                turn_tile(0, 0, 0)
                for u in range(1, U):
                    turn_tile(u, u, 0)
                    multiply(u - 1, (u - 1) % 2)
                with pe.Fori(1, FULL, 1) as i:
                    for u in range(U):
                        turn_tile(U * i + u, u, i)
                        multiply(U * i + u - 1, (u - 1) % 2)
                for u in range(TTILES - U * FULL):
                    turn_tile(U * FULL + u, u, FULL)
                    multiply(U * FULL + u - 1, (u - 1) % 2)
                multiply(TTILES - 1, (TTILES - 1) % 2)


def gnn_ffn(nc, x, src, dst, edge_weight, gnn_eps, gnn_w1, gnn_b1, gnn_g1, gnn_be1, gnn_w2, gnn_b2, gnn_g2, gnn_be2,
            ffn_w1, ffn_b1, ffn_wg, ffn_bg, ffn_wd, ffn_bd, out):
    table = nc.dram_tensor("node_table", [ROWS, D], F32).ap()
    accs = [nc.dram_tensor(f"accumulator{k}", [ROWS, D], F32).ap() for k in range(STREAMS)]
    halves = nc.dram_tensor("target_halves", [2, ECOLS * P], BF16).ap()
    regions = nc.dram_tensor("regions", [REGION_ROWS, PAY], F32).ap()
    with ExitStack() as whole:
        m = Memory(nc, whole, "all")
        c = Constants(m)
        ends = m.sb("ends", [P, NE], I32)
        scale = m.sb("scale", [P, DH])
        shift = m.sb("shift", [P, DH])
        with ExitStack() as ctx:
            e = Memory(nc, ctx, "edges")
            edge_cols = e.sb("cols", [P, EGROUPS, 4, G])
            bases = e.sb("bases", [1, EGROUPS], I32)
            flag = e.sb("flag", [P, 1], I32)
            prepare(nc, c, x, src, dst, edge_weight, gnn_eps, table, accs, halves, edge_cols, bases, flag)
            add_edges(nc, c, table, accs, halves, edge_cols, bases, flag)
        with ExitStack() as ctx:
            hid = Memory(nc, ctx, "nodes").sb("hid", [P, DH, NPAD])
            linear(nc, c, accs, gnn_w1, gnn_b1, gnn_g1, gnn_be1, gnn_w2, gnn_b2, gnn_g2, gnn_be2, hid, scale, shift)
            gate(nc, c, x, ffn_w1, ffn_b1, ffn_wg, ffn_bg, hid, scale, shift, regions, ends)
        experts(nc, c, ffn_wd, ffn_bd, regions, ends, out)


_INS = ['x', 'src', 'dst', 'edge_weight', 'L0_gnn_eps', 'L0_gnn_W1', 'L0_gnn_b1', 'L0_gnn_g1', 'L0_gnn_be1',
        'L0_gnn_W2', 'L0_gnn_b2', 'L0_gnn_g2', 'L0_gnn_be2', 'L0_ffn_W1', 'L0_ffn_b1', 'L0_ffn_Wg', 'L0_ffn_bg',
        'L0_ffn_Wd', 'L0_ffn_bd']


def kernel(**inputs):
    import numpy as _np
    import concourse.bacc as _bacc
    from concourse.bass_utils import run_bass_kernel_spmd as _run

    nc = _bacc.Bacc("TRN2", target_bir_lowering=False, num_devices=1)
    arrays, args = {}, []
    for name in _INS:
        a = _np.ascontiguousarray(inputs[name])
        arrays[f"in_{name}_dram"] = a
        args.append(nc.dram_tensor(f"in_{name}_dram", a.shape, mybir.dt.from_np(a.dtype), kind="ExternalInput").ap())
    args.append(nc.dram_tensor("out_0_dram", [N, D], F32, kind="ExternalOutput").ap())
    gnn_ffn(nc, *args)
    return _run(nc, [arrays], core_ids=[0]).results[0]["out_0_dram"]
```

```python
from contextlib import ExitStack

import concourse.bass as bass
from concourse import mybir

F32 = mybir.dt.float32
F32R = mybir.dt.float32r
BF16 = mybir.dt.bfloat16
I32 = mybir.dt.int32
ALU = mybir.AluOpType
ACT = mybir.ActivationFunctionType
AX = mybir.AxisListType

P = 128
N = 12500
E = 200000
D = 256
DH = D // P
HID = 1024
KC = HID // P
NE = 8
EPS = 1e-5

CH = 4
CN = CH * P
NCH = -(-N // CN)
NPAD = NCH * CN
LAST = NCH - 1
DUMMY = NPAD
ROWS = NPAD + P
STREAMS = 4
ZRUNS = 16

G = 8
GE = G * P
ETILES = -(-E // P)
EB = -(-ETILES // P)
ECOLS = EB * P
EGROUPS = ECOLS // G
PAIRS = -(-ETILES // (2 * G))
GROUPS = 2 * PAIRS
FULL_BLOCKS = E // (P * P)
REST = E - FULL_BLOCKS * P * P
REST_ROWS = REST // P
REST_LAST = REST % P

CAP = -(-(N + 2 * (P - 1)) // 8) * 8
PAIRS_E = NE // 2
NOWHERE = PAIRS_E * CAP
STRAY = NOWHERE + P
REGION_ROWS = STRAY + CN
PAY_X = HID
PAY_GATE = HID + D
PAY_TOKEN = PAY_GATE + NE
PAY = PAY_TOKEN + 4
NO_TOKEN = 1 << 20
TTILES = N // P + NE
RESIDUAL_AT = 0
TURN_LOGITS_AT = 1
CHOOSE_AT = 1
MOMENTS_AT = 2
COUNT_AT = 3
PLACE_AT = 3
NORMALISE_AT = 4
XN_AT = 5


def ds(start, size):
    return bass.ds(start, size)


class Steps:

    def __init__(self, eng, sem):
        self.eng, self.sem, self.n = eng, sem, 0

    def restart(self):
        self.eng.sem_clear(self.sem)
        self.n = 0

    def link(self, ins):
        self.n += 1
        ins.then_inc(self.sem, 1)
        self.eng.wait_ge(self.sem, self.n)


ROOT_GUESS = float(0x5F3759DF)


def inverse_root(dve, steps, v, root, work, variance):
    steps.link(dve.tensor_scalar(v, variance, EPS, None, ALU.add))
    steps.link(dve.tensor_scalar(root.bitcast(I32), v.bitcast(I32), 1, None, ALU.arith_shift_right))
    steps.link(dve.tensor_scalar(root.bitcast(I32), root.bitcast(I32), -1.0, ROOT_GUESS, ALU.mult, ALU.add))
    for _ in range(3):
        steps.link(dve.scalar_tensor_tensor(work, root, -0.5, root, ALU.mult, ALU.mult))
        steps.link(dve.tensor_tensor(work, work, v, ALU.mult))
        steps.link(dve.scalar_tensor_tensor(root, work, 1.5, root, ALU.add, ALU.mult))


class Memory:

    def __init__(self, nc, ctx, phase):
        self.nc, self.ctx, self.phase = nc, ctx, phase

    def sb(self, name, shape, dt=F32):
        return self.ctx.enter_context(self.nc.sbuf_tensor(f"{self.phase}_{name}", shape, dt))

    def ps(self, name, shape, dt=F32):
        return self.ctx.enter_context(self.nc.psum_tensor(f"{self.phase}_{name}", shape, dt))

    def sem(self, name):
        return self.ctx.enter_context(self.nc.semaphore(f"{self.phase}_{name}"))


def prepare(nc, c, x, src, dst, weight, gnn_eps, table, accs, halves, edge_cols, bases, flag):
    with ExitStack() as ctx:
        m = Memory(nc, ctx, "prep")
        xt = m.sb("xt", [P, 2, CH, D])
        xn = m.sb("xn", [P, 2, CH, D])
        own = m.sb("own", [P, 2, CH, D])
        stats = m.sb("stats", [P, CH, 6])
        mv = m.sb("mv", [P, 2, CH, 2])
        var = m.sb("var", [P, CH, 1])
        std = m.sb("std", [P, 2, CH, 1])
        rstd = m.sb("rstd", [P, CH, 1])
        eps1 = m.sb("eps1", [P, 1])
        eps_in = m.sb("eps_in", [P, 1])
        zeros = m.sb("zeros", [P, ROWS * D // P // ZRUNS])
        nsrc = m.sb("nsrc", [P, EB, P], I32)
        ndst = m.sb("ndst", [P, EB, P], I32)
        nw = m.sb("nw", [P, EB, P])
        nhalf = m.sb("nhalf", [P, EB, P], I32)
        nhi = m.sb("nhi", [P, EB, P], BF16)
        nlo = m.sb("nlo", [P, EB, P], BF16)
        nf = m.sb("nf", [P, EB, P])
        ng = m.sb("ng", [P, EB, P])
        dcol = m.sb("dcol", [P, ECOLS])
        bad = m.sb("bad", [P, EGROUPS, G])
        bad1 = m.sb("bad1", [P, 1])
        ramp = m.sb("ramp", [P, P], I32)
        line = m.sb("line", [P, P], I32)
        down = m.sb("down", [P, 1], I32)
        rev = m.sb("rev", [P, NE], I32)
        turned = m.ps("turned", [P, 2048])
        turned2 = m.ps("turned2", [P, 2048])

        x_in = [m.sem(f"x_in{s}") for s in range(2)]
        edge_in = m.sem("edge_in")
        eps_sem = m.sem("eps_in")
        zero_set = m.sem("zero_set")
        pads_set = m.sem("pads_set")
        slot_set = m.sem("slot_set")
        consts = m.sem("consts")
        iotas = m.sem("iotas")
        var_ready = m.sem("var_ready")
        std_ready = m.sem("std_ready")
        xn_ready = m.sem("xn_ready")
        own_ready = m.sem("own_ready")
        xn_out = [m.sem(f"xn_out{s}") for s in range(2)]
        own_out = [m.sem(f"own_out{s}") for s in range(2)]
        zero_out = m.sem("zero_out")
        half_ready = m.sem("half_ready")
        half_out = m.sem("half_out")
        flat_ready = m.sem("flat_ready")
        turned_ready = m.sem("turned_ready")
        turned_free = m.sem("turned_free")
        bad_ready = m.sem("bad_ready")
        flag_sum = m.sem("flag_sum")
        steps_sem = m.sem("steps")

        def chunk(t, i):
            return t[ds(i * CN, CN), :].rearrange("(j p) f -> p j f", p=P)

        def blocks(a):
            return a[0:FULL_BLOCKS * P * P].rearrange("(b q e) -> q b e", q=P, e=P)

        with nc.Block() as block:

            @block.sync
            def _(sp):
                sp.wait_ge(pads_set, 3)
                for to, a in ((nsrc, src), (ndst, dst), (nw, weight)):
                    sp.dma_start(to[:, 0:FULL_BLOCKS, :], blocks(a)).then_inc(edge_in, 16)
                    rest = a[FULL_BLOCKS * P * P:FULL_BLOCKS * P * P + REST_ROWS * P]
                    sp.dma_start(to[0:REST_ROWS, FULL_BLOCKS, :],
                                 rest.rearrange("(q e) -> q e", e=P)).then_inc(edge_in, 16)
                    if REST_LAST:
                        sp.dma_start(to[REST_ROWS:REST_ROWS + 1, FULL_BLOCKS, 0:REST_LAST],
                                     a[E - REST_LAST:E].rearrange("(q e) -> q e", q=1)).then_inc(edge_in, 16)

                def load(i, s):
                    sp.dma_start(xt[:, s, :, :], chunk(x, i)).then_inc(x_in[s], 16)

                load(0, 0)
                load(1, 1)
                with sp.Fori(1, LAST // 2, 1) as i:
                    for s in range(2):
                        sp.wait_ge(xn_ready, 2 * i + s - 1)
                        load(2 * i + s, s)
                sp.wait_ge(slot_set, 1)
                full = (N - LAST * CN) // P
                part = (N - LAST * CN) % P
                sp.dma_start(xt[:, 0, 0:full, :],
                             x[LAST * CN:LAST * CN + full * P, :].rearrange("(j p) f -> p j f", p=P)).then_inc(x_in[0], 16)
                sp.dma_start(xt[0:part, 0, full, :], x[N - part:N, :]).then_inc(x_in[0], 16)
                sp.wait_ge(zero_set, 1)
                for t in accs[1:]:
                    sp.dma_start(t.rearrange("(p r) f -> p (r f)", p=P).rearrange("p (z w) -> p z w", z=ZRUNS),
                                 zeros[:].unsqueeze(1).to_broadcast([P, ZRUNS, ROWS * D // P // ZRUNS])).then_inc(zero_out, 16)
                for t in (table, accs[0]):
                    sp.dma_start(t[NPAD:ROWS, :], zeros[:, 0:D]).then_inc(zero_out, 16)
                sp.wait_ge(half_ready, 2)
                for h, half in enumerate((nhi, nlo)):
                    sp.dma_start(halves[h:h + 1, :].rearrange("o (b q e) -> (o q) b e", q=P, e=P),
                                 half[:, :, :]).then_inc(half_out, 16)
                sp.wait_ge(zero_out, 16 * (STREAMS - 1 + 2))
                sp.wait_ge(half_out, 32)

            @block.gpsimd
            def _(pool):
                for t in (nsrc, ndst, nw):
                    pool.memset(t[:, FULL_BLOCKS:EB, :], 0).then_inc(pads_set, 1)
                pool.dma_start(eps_in[:], gnn_eps.partition_broadcast(P)).then_inc(eps_sem, 16)
                pool.memset(zeros[:], 0.0).then_inc(zero_set, 1)
                pool.iota(ramp[:], [[1, P]], base=0, channel_multiplier=-1).then_inc(iotas, 1)
                pool.iota(line[:], [[1, P]], base=0, channel_multiplier=0).then_inc(iotas, 1)
                pool.iota(down[:], [[0, 1]], base=0, channel_multiplier=1).then_inc(iotas, 1)
                pool.iota(rev[:], [[-1, NE]], base=NE, channel_multiplier=0).then_inc(iotas, 1)

            @block.scalar
            def _(act):
                act.wait_ge(consts, 1)

                def turn(i, s, before):
                    act.wait_ge(var_ready, i + 1)
                    act.activation(std[:, s], var[:], ACT.Sqrt).then_inc(std_ready, 1)
                    act.wait_ge(xn_ready, i + 1)
                    act.dma_start(chunk(table, i), xn[:, s]).then_inc(xn_out[s], 16)
                    if not isinstance(i, int) or i >= 2:
                        act.wait_ge(own_out[s], 16 * before)
                    act.activation(own[:, s], xn[:, s], ACT.Identity, scale=eps1[:, 0:1]).then_inc(own_ready, 1)
                    act.wait_ge(own_ready, i + 1)
                    act.dma_start(chunk(accs[0], i), own[:, s]).then_inc(own_out[s], 16)

                turn(0, 0, 0)
                turn(1, 1, 0)
                with act.Fori(1, LAST // 2, 1) as i:
                    turn(2 * i, 0, i)
                    turn(2 * i + 1, 1, i)
                turn(LAST, 0, LAST // 2)
                for s in range(2):
                    act.wait_ge(xn_out[s], 16 * (LAST // 2 + 1 - s))
                    act.wait_ge(own_out[s], 16 * (LAST // 2 + 1 - s))

            @block.vector
            def _(dve):
                steps = Steps(dve, steps_sem)
                dve.wait_ge(iotas, 4)
                dve.tensor_scalar(c.ident[:], ramp[:], 0.0, None, ALU.is_equal)
                dve.tensor_scalar(c.before[:], ramp[:], 0.0, None, ALU.is_lt)
                dve.tensor_scalar(c.after[:], ramp[:], 0.0, None, ALU.is_gt)
                dve.tensor_copy(c.line[:], line[:])
                dve.tensor_scalar(c.dummy[:], down[:], float(DUMMY), None, ALU.add)
                dve.tensor_copy(c.down[:], down[:])
                dve.tensor_copy(c.rev[:], rev[:])
                dve.memset(c.ones[:], 1.0)
                dve.memset(c.ones16[:], 1.0)
                dve.wait_ge(eps_sem, 16)
                dve.tensor_scalar(eps1[:], eps_in[:], 1.0, None, ALU.add).then_inc(consts, 1)
                dve.memset(c.joins[0:2, :], 1.0).then_inc(steps_sem, 1)
                dve.wait_ge(steps_sem, 1)
                dve.memset(c.joins[0:1, :], float(P)).then_inc(steps_sem, 1)
                dve.wait_ge(steps_sem, 2)

                dve.wait_ge(edge_in, 16 * 3 * (3 if REST_LAST else 2))
                steps.restart()
                steps.link(dve.tensor_scalar(nhalf[:], nsrc[:], 7, None, ALU.arith_shift_right))
                steps.link(dve.tensor_copy(nhi[:], nhalf[:]))
                dve.sem_inc(half_ready, 1)
                steps.link(dve.tensor_scalar(nhalf[:], nsrc[:], P - 1, None, ALU.bitwise_and))
                steps.link(dve.tensor_copy(nlo[:], nhalf[:]))
                dve.sem_inc(half_ready, 1)
                dve.tensor_copy(nf[:], nsrc[:]).then_inc(flat_ready, 1)
                dve.tensor_copy(ng[:], ndst[:]).then_inc(flat_ready, 1)

                def turn(i, s, before):
                    steps.restart()
                    dve.wait_ge(x_in[s], 16 * (before + 1) if not isinstance(i, int) or i < LAST else 16 * (before + 2))
                    for j in range(CH):
                        last = dve.bn_stats(stats[:, j, :], xt[:, s, j, :])
                    steps.link(last)
                    for j in range(CH):
                        last = dve.bn_aggr(mv[:, s, j, :], stats[:, j, :])
                    steps.link(last)
                    dve.tensor_scalar(var[:], mv[:, s, :, 1:2], EPS, None, ALU.add).then_inc(var_ready, 1)
                    dve.wait_ge(std_ready, i + 1)
                    steps.link(dve.reciprocal(rstd[:], std[:, s]))
                    if not isinstance(i, int) or i >= 2:
                        dve.wait_ge(xn_out[s], 16 * before)
                        dve.wait_ge(own_ready, i - 1)
                    for j in range(CH):
                        last = dve.tensor_scalar(xn[:, s, j, :], xt[:, s, j, :], mv[:, s, j, 0:1],
                                                 rstd[:, j, 0:1], ALU.subtract, ALU.mult)
                    last.then_inc(xn_ready, 1)

                turn(0, 0, 0)
                turn(1, 1, 0)
                with dve.Fori(1, LAST // 2, 1) as i:
                    turn(2 * i, 0, i)
                    turn(2 * i + 1, 1, i)
                dve.wait_ge(xn_ready, LAST)
                dve.memset(xt[:, 0], 0.0).then_inc(slot_set, 1)
                turn(LAST, 0, LAST // 2)

                dve.wait_ge(turned_ready, 1)
                dve.tensor_copy(edge_cols[:, :, 0, :], turned[:, 0:ECOLS].rearrange("p (g t) -> p g t", t=G)).then_inc(turned_free, 1)
                dve.wait_ge(turned_ready, 2)
                steps.restart()
                steps.link(dve.tensor_copy(dcol[:], turned2[:, 0:ECOLS]))
                dve.sem_inc(turned_free, 1)
                dve.wait_ge(turned_ready, 3)
                dve.tensor_copy(edge_cols[:, :, 2, :], turned[:, 0:ECOLS].rearrange("p (g t) -> p g t", t=G))
                dve.tensor_copy(edge_cols[:, :, 3, :], dcol[:].rearrange("p (g t) -> p g t", t=G))
                dve.wait_ge(turned_ready, 4)
                first = turned2[:, 0:EGROUPS]
                dve.tensor_copy(bases[0:1, :], turned2[0:1, 0:EGROUPS])
                steps.link(dve.tensor_tensor(edge_cols[:, :, 1, :], dcol[:].rearrange("p (g t) -> p g t", t=G),
                                             first.unsqueeze(2).to_broadcast([P, EGROUPS, G]), ALU.subtract))
                tile, row = divmod(E, P)
                if row:
                    dve.memset(edge_cols[row:P, tile // G, 1, tile % G:tile % G + 1], 0.0)
                    tile += 1
                if tile % G:
                    dve.memset(edge_cols[:, tile // G, 1, tile % G:G], 0.0)
                    tile += G - tile % G
                steps.link(dve.memset(edge_cols[:, tile // G:EGROUPS, 1, :], 0.0))
                local = edge_cols[:, :, 1, :]
                steps.link(dve.tensor_scalar(bad[:], local, float(P - 1), None, ALU.is_gt))
                steps.link(dve.scalar_tensor_tensor(bad[:], local, 0.0, bad[:], ALU.is_lt, ALU.add))
                dve.tensor_reduce(bad1[:], bad[:].rearrange("p g t -> p (g t)"), AX.X, ALU.add).then_inc(bad_ready, 1)
                dve.wait_ge(flag_sum, 1)
                steps.link(dve.tensor_scalar(bad1[:], turned[:, 0:1], 0.0, None, ALU.is_gt))
                steps.link(dve.tensor_copy(flag[:], bad1[:]))

            @block.tensor
            def _(pe):
                def turn(to, a):
                    for b in range(EB):
                        last = pe.transpose(to[:, b * P:(b + 1) * P], a[:, b, :], c.ident[:])
                    last.then_inc(turned_ready, 1)

                pe.wait_ge(flat_ready, 2)
                turn(turned, nf)
                turn(turned2, ng)
                pe.wait_ge(turned_free, 1)
                turn(turned, nw)
                pe.wait_ge(turned_free, 2)
                pe.matmul(turned2[:, 0:EGROUPS], c.ones[0:1, :],
                          dcol[0:1, :].rearrange("p (g t) -> p g t", t=G)[:, :, 0],
                          start=True, stop=True).then_inc(turned_ready, 1)
                pe.wait_ge(bad_ready, 1)
                pe.matmul(turned[:, 0:1], c.ones[:, :], bad1[:, :], start=True, stop=True).then_inc(flag_sum, 1)


def add_edges(nc, c, table, accs, halves, edge_cols, bases, flag):
    with ExitStack() as ctx:
        m = Memory(nc, ctx, "edge")
        rows = m.sb("rows", [2, 2, GE], BF16)
        window = m.sb("window", [P, 2, D])
        cols = m.sb("cols", [P, 2, 4, G])
        same = m.sb("same", [P, 2, G, P])
        pick = m.sb("pick", [P, 2, G, P])
        earlier = m.sb("earlier", [P, G, P])
        nearlier = m.sb("nearlier", [P, G])
        move = m.sb("move", [P, G])
        target = m.sb("target", [P, 2, G], I32)
        node = m.sb("node", [P, 2, G], I32)
        mix = m.sb("mix", [P, 2, G, P])
        gathered = m.sb("gathered", [P, 2, G, D])
        sums = m.sb("sums", [P, 2, G, D])
        ps_rows = m.ps("ps_rows", [P, G, P])
        ps_mix = m.ps("ps_mix", [P, G, P])
        ps_sums = m.ps("ps_sums", [P, G // 2, 2, D])

        rows_in = [m.sem(f"rows_in{s}") for s in range(2)]
        window_in = [m.sem(f"window_in{s}") for s in range(2)]
        rows_done = m.sem("rows_done")
        same_ready = m.sem("same_ready")
        pick_ready = m.sem("pick_ready")
        target_ready = m.sem("target_ready")
        mix_done = m.sem("mix_done")
        mix_ready = m.sem("mix_ready")
        sums_done = m.sem("sums_done")
        sums_ready = m.sem("sums_ready")
        added = [m.sem(f"added{k}") for k in range(STREAMS)]
        gather_in = m.sem("gather_in")
        pool_turn = m.sem("pool_turn")
        act_turn = m.sem("act_turn")
        sp_turn = m.sem("sp_turn")
        steps_sem = m.sem("steps")
        QUADS = G // 2
        PER = G // STREAMS

        def later(i, by):
            return not isinstance(i, int) or i >= by

        def all_pairs(eng, group):
            group(0, 0)
            group(1, 1)
            with eng.Fori(1, PAIRS, 1) as i:
                group(2 * i, 0)
                group(2 * i + 1, 1)

        with nc.Block() as block:

            @block.sync
            def _(sp):
                general = sp.value_load(flag[0:1, 0:1], min_val=0, max_val=1)

                def load_rows(i, s):
                    if later(i, 2):
                        sp.wait_ge(rows_done, i - 1)
                    sp.dma_start(rows[:, s, :], halves[:, ds(i * GE, GE)]).then_inc(rows_in[s], 16)

                def group(i, s, fast):
                    load_rows(i, s)
                    if fast:
                        if later(i, 2):
                            sp.wait_ge(sums_done, QUADS * (i - 1))
                            sp.sem_inc(sp_turn, 1)
                        base = sp.value_load(bases[0:1, ds(i, 1)], min_val=0, max_val=N - 1)
                        sp.dma_start(window[:, s, :], table[ds(base, P), :]).then_inc(window_in[s], 16)

                with sp.If(general):
                    all_pairs(sp, lambda i, s: group(i, s, False))
                    load_rows(GROUPS, 0)
                with sp.Else():
                    all_pairs(sp, lambda i, s: group(i, s, True))
                    load_rows(GROUPS, 0)
                sp.wait_ge(rows_in[0], 16 * (PAIRS + 1))

            @block.gpsimd
            def _(pool):
                general = pool.value_load(flag[0:1, 0:1], min_val=0, max_val=1)

                def gather(i, s):
                    pool.wait_ge(target_ready, i + 1)
                    if later(i, 2):
                        pool.wait_ge(sums_done, QUADS * (i - 1))
                    pool.sem_inc(pool_turn, 1)
                    for t in range(G):
                        pool.indirect_dma_start(
                            out=gathered[:, s, t, :], out_offset=None, in_=table[:, :],
                            in_offset=bass.IndirectOffsetOnAxis(ap=node[:, s, t:t + 1], axis=0),
                        ).then_inc(gather_in, 16)

                def group(i, s, fast):
                    if not fast:
                        gather(i, s)
                    for t in range(G):
                        if t == 0:
                            pool.wait_ge(target_ready, i + 1)
                        if t % 2 == 0:
                            pool.wait_ge(sums_ready, QUADS * i + t // 2 + 1)
                        if later(i, 1) or t >= STREAMS:
                            pool.wait_ge(added[t % STREAMS], 16 * (PER * i + t // STREAMS))
                        pool.sem_inc(pool_turn, 1)
                        pool.indirect_dma_start(
                            out=accs[t % STREAMS][:, :],
                            out_offset=bass.IndirectOffsetOnAxis(ap=target[:, s, t:t + 1], axis=0),
                            in_=sums[:, s, t, :], in_offset=None, compute_op=ALU.add,
                        ).then_inc(added[t % STREAMS], 16)

                with pool.If(general):
                    all_pairs(pool, lambda i, s: group(i, s, False))
                with pool.Else():
                    all_pairs(pool, lambda i, s: group(i, s, True))
                for k in range(STREAMS):
                    pool.wait_ge(added[k], 16 * PER * GROUPS)

            @block.vector
            def _(dve):
                general = dve.value_load(flag[0:1, 0:1], min_val=0, max_val=1)
                steps = Steps(dve, steps_sem)

                def group(i, s, fast):
                    steps.restart()
                    if later(i, 2):
                        dve.wait_ge(sums_done if not fast else mix_done, (QUADS if not fast else 1) * (i - 1))
                    steps.link(dve.tensor_copy(cols[:, s, :, :], edge_cols[:, ds(i, 1), :, :].rearrange("p o a t -> p (o a) t")))
                    target_f, local, wt, node_f = (cols[:, s, a, :] for a in range(4))
                    dve.wait_ge(rows_done, i + 1)
                    ins = dve.tensor_tensor(same[:, s], ps_rows[:, :, :],
                                            target_f.unsqueeze(2).to_broadcast([P, G, P]), ALU.is_equal)
                    ins.then_inc(same_ready, 1)
                    dve.wait_ge(same_ready, i + 1)
                    if fast:
                        for t in range(G):
                            ins = dve.tensor_scalar(pick[:, s, t, :], c.line[:], local[:, t:t + 1], wt[:, t:t + 1],
                                                    ALU.is_equal, ALU.mult)
                    else:
                        for t in range(G):
                            ins = dve.tensor_scalar(pick[:, s, t, :], same[:, s, t, :], wt[:, t:t + 1], None, ALU.mult)
                        dve.tensor_copy(node[:, s, :], node_f)
                    ins.then_inc(pick_ready, 1)
                    steps.link(dve.tensor_tensor(earlier[:], same[:, s],
                                                 c.before[:].unsqueeze(1).to_broadcast([P, G, P]), ALU.mult))
                    dve.tensor_reduce(nearlier[:], earlier[:], AX.X, ALU.add)
                    steps.link(dve.tensor_scalar(move[:], target_f, -1.0, c.dummy[:, 0:1], ALU.mult, ALU.add))
                    steps.link(dve.scalar_tensor_tensor(move[:], nearlier[:], 1.0, move[:], ALU.min, ALU.mult))
                    if later(i, 2):
                        for k in range(STREAMS):
                            dve.wait_ge(added[k], 16 * PER * (i - 1))
                    steps.link(dve.tensor_tensor(target[:, s, :], move[:], target_f, ALU.add))
                    dve.sem_inc(target_ready, 1)

                with dve.If(general):
                    all_pairs(dve, lambda i, s: group(i, s, False))
                with dve.Else():
                    all_pairs(dve, lambda i, s: group(i, s, True))

            @block.tensor
            def _(pe):
                general = pe.value_load(flag[0:1, 0:1], min_val=0, max_val=1)

                def weigh(i, s):
                    pe.wait_ge(pick_ready, i + 1)
                    if later(i, 1):
                        pe.wait_ge(mix_ready, i)
                    for t in range(G):
                        ins = pe.matmul(ps_mix[:, t, :], pick[:, s, t, :], same[:, s, t, :], start=True, stop=True)
                    ins.then_inc(mix_done, 1)

                def add_up(i, s, turns, fast):
                    if fast:
                        pe.wait_ge(mix_ready, i + 1)
                        pe.wait_ge(window_in[s], 16 * turns)
                    else:
                        pe.wait_ge(pick_ready, i + 1)
                        pe.wait_ge(gather_in, 16 * G * (i + 1))
                    for q in range(QUADS):
                        if later(i, 1):
                            pe.wait_ge(sums_ready, QUADS * (i - 1) + q + 1)
                        for u in range(2):
                            t = 2 * q + u
                            ins = pe.matmul(ps_sums[:, q, u, :], (mix if fast else pick)[:, s, t, :],
                                            window[:, s, :] if fast else gathered[:, s, t, :], start=True, stop=True)
                        ins.then_inc(sums_done, 1)

                def rows_of(i, s, turns):
                    pe.wait_ge(rows_in[s], 16 * turns)
                    if later(i, 1):
                        pe.wait_ge(same_ready, i)
                    for b in range(2):
                        ins = pe.matmul(ps_rows[:, b * (G // 2):(b + 1) * (G // 2), :], c.joins[:, :],
                                        rows[:, s, b * 512:(b + 1) * 512], start=True, stop=True)
                    ins.then_inc(rows_done, 1)

                def pair(p, fast):
                    for s in range(2):
                        i = 2 * p + s
                        rows_of(i + 1, 1 - s, p + 1 if s == 0 else p + 2)
                        if fast:
                            if later(i, 1):
                                add_up(i - 1, 1 - s, p if s == 0 else p + 1, fast)
                            weigh(i, s)
                        else:
                            add_up(i, s, p + 1, fast)

                def all_groups(fast):
                    rows_of(0, 0, 1)
                    pair(0, fast)
                    with pe.Fori(1, PAIRS, 1) as p:
                        pair(p, fast)
                    if fast:
                        add_up(GROUPS - 1, 1, PAIRS, fast)

                with pe.If(general):
                    all_groups(False)
                with pe.Else():
                    all_groups(True)

            @block.scalar
            def _(act):
                general = act.value_load(flag[0:1, 0:1], min_val=0, max_val=1)

                def group_mix(i, s):
                    act.wait_ge(mix_done, i + 1)
                    if later(i, 2):
                        act.wait_ge(sums_done, QUADS * (i - 1))
                    act.activation(mix[:, s], ps_mix[:, :, :], ACT.Copy).then_inc(mix_ready, 1)

                def group_sums(i, s):
                    for q in range(QUADS):
                        act.wait_ge(sums_done, QUADS * i + q + 1)
                        if later(i, 2) and q == 0:
                            for k in range(STREAMS):
                                act.wait_ge(added[k], 16 * PER * (i - 1))
                        act.activation(sums[:, s, 2 * q:2 * q + 2, :], ps_sums[:, q, :, :], ACT.Copy).then_inc(sums_ready, 1)

                with act.If(general):
                    all_pairs(act, group_sums)
                with act.Else():
                    group_mix(0, 0)
                    group_sums(0, 0)
                    group_mix(1, 1)
                    with act.Fori(1, PAIRS, 1) as p:
                        for s in range(2):
                            group_sums(2 * p + s - 1, 1 - s)
                            group_mix(2 * p + s, s)
                    group_sums(GROUPS - 1, 1)


class Constants:

    def __init__(self, m):
        self.ident = m.sb("ident", [P, P])
        self.after = m.sb("after", [P, P], BF16)
        self.rev = m.sb("rev", [P, NE])
        self.ones16 = m.sb("ones16", [P, P], BF16)

    def for_edges(self, m):
        self.before = m.sb("before", [P, P])
        self.line = m.sb("line", [P, P])
        self.down = m.sb("down", [P, 1])
        self.dummy = m.sb("dummy", [P, 1])
        self.ones = m.sb("ones", [P, P])
        self.joins = m.sb("joins", [2, P], BF16)


def linear(nc, c, accs, w1, b1, g1, be1, w2, b2, g2, be2, hid, scale, shift):
    with ExitStack() as ctx:
        m = Memory(nc, ctx, "lin")
        parts = m.sb("parts", [P, 2, STREAMS, CH, D])
        hT = m.sb("hT", [P, 2, DH, CN])
        w_sb = m.sb("w_sb", [P, 2, DH, D])
        vec = m.sb("vec", [P, 2, 3, DH])
        stats = m.sb("stats", [P, DH, NCH, 6])
        mv = m.sb("mv", [P, DH, 2])
        std = m.sb("std", [P, DH])
        sc1 = m.sb("sc1", [P, DH])
        sh1 = m.sb("sh1", [P, DH])
        tmp = m.sb("tmp", [P, DH])
        ps_t = m.ps("ps_t", [P, 2, DH, CN])
        ps_h = m.ps("ps_h", [P, 2, DH, CN])

        params_in = m.sem("params_in")
        parts_in = [m.sem(f"parts_in{s}") for s in range(2)]
        sum_ready = m.sem("sum_ready")
        turned = m.sem("turned")
        hT_ready = m.sem("hT_ready")
        hid_done = m.sem("hid_done")
        hid_ready = m.sem("hid_ready")
        var_ready = m.sem("var_ready")
        std_ready = m.sem("std_ready")
        norm_ready = m.sem("norm_ready")
        act_turn = m.sem("act_turn")
        dve_turn = m.sem("dve_turn")
        sp_turn = m.sem("sp_turn")
        steps_sem = m.sem("steps")

        def columns(i, h):
            return hid[:, ds(i, 1), h, :].rearrange("p o n -> p (o n)")

        def all_chunks(eng, chunk):
            chunk(0, 0, 0)
            chunk(1, 1, 0)
            with eng.Fori(1, LAST // 2, 1) as i:
                chunk(2 * i, 0, i)
                chunk(2 * i + 1, 1, i)
            chunk(LAST, 0, LAST // 2)

        def second(i):
            return not isinstance(i, int) or i >= 2

        with nc.Block() as block:

            @block.sync
            def _(sp):
                for a, (w, vs) in enumerate(((w1, (b1, g1, be1)), (w2, (b2, g2, be2)))):
                    sp.dma_start(w_sb[:, a, :, :], w.rearrange("(k p) o -> p k o", p=P)).then_inc(params_in, 16)
                    for b, v in enumerate(vs):
                        for h in range(DH):
                            sp.dma_start(vec[:, a, b, h:h + 1], v[h * P:(h + 1) * P].rearrange("(p o) -> p o", o=1)).then_inc(params_in, 16)

                def chunk(i, s, before):
                    if second(i):
                        sp.wait_ge(turned, i - 1)
                        sp.sem_inc(sp_turn, 1)
                    for k in range(STREAMS):
                        sp.dma_start(parts[:, s, k, :, :],
                                     accs[k][ds(i * CN, CN), :].rearrange("(j p) f -> p j f", p=P)).then_inc(parts_in[s], 16)

                all_chunks(sp, chunk)

            @block.vector
            def _(dve):
                steps = Steps(dve, steps_sem)

                def records(i, base):
                    dve.wait_ge(hid_ready, DH * (base + i + 1))
                    dve.sem_inc(dve_turn, 1)
                    nodes = N - LAST * CN if isinstance(i, int) and i == LAST else CN
                    for h in range(DH):
                        ins = dve.bn_stats(stats[:, h, ds(i, 1), :].rearrange("p o r -> p (o r)"), columns(i, h)[:, 0:nodes])
                    return ins

                def chunk1(i, s, before):
                    steps.restart()
                    dve.wait_ge(parts_in[s], 16 * STREAMS * (before + 1))
                    for k in range(1, STREAMS - 1):
                        steps.link(dve.tensor_tensor(parts[:, s, 0], parts[:, s, 0], parts[:, s, k], ALU.add))
                    dve.tensor_tensor(parts[:, s, 0], parts[:, s, 0], parts[:, s, STREAMS - 1], ALU.add).then_inc(sum_ready, 1)
                    if second(i):
                        records(i - 2, 0)

                def affine(a, sc, sh, base):
                    steps.restart()
                    records(LAST - 1, base)
                    steps.link(records(LAST, base))
                    for h in range(DH):
                        ins = dve.bn_aggr(mv[:, h, :], stats[:, h, :, :].rearrange("p c r -> p (c r)"))
                    steps.link(ins)
                    dve.tensor_scalar(tmp[:], mv[:, :, 1], EPS, None, ALU.add).then_inc(var_ready, 1)
                    dve.wait_ge(std_ready, a + 1)
                    steps.link(dve.reciprocal(tmp[:], std[:]))
                    steps.link(dve.tensor_tensor(sc[:], tmp[:], vec[:, a, 1, :], ALU.mult))
                    steps.link(dve.tensor_tensor(tmp[:], mv[:, :, 0], sc[:], ALU.mult))
                    steps.link(dve.tensor_tensor(sh[:], vec[:, a, 2, :], tmp[:], ALU.subtract))
                    dve.sem_inc(norm_ready, 1)

                dve.wait_ge(params_in, 16 * 2 * (1 + 3 * DH))
                all_chunks(dve, chunk1)
                affine(0, sc1, sh1, 0)
                dve.wait_ge(hid_ready, DH * NCH)
                with dve.Fori(0, LAST - 1, 1) as i:
                    records(i, NCH)
                affine(1, scale, shift, NCH)

            @block.tensor
            def _(pe):
                pe.wait_ge(params_in, 16 * 2 * (1 + 3 * DH))

                def turn(i, s):
                    pe.wait_ge(sum_ready, i + 1)
                    if second(i):
                        pe.wait_ge(hT_ready, i - 1)
                    for h in range(DH):
                        for j in range(CH):
                            ins = pe.transpose(ps_t[:, s, h, j * P:(j + 1) * P], parts[:, s, 0, j, h * P:(h + 1) * P], c.ident[:])
                    ins.then_inc(turned, 1)

                def layer(i, s, a, base):
                    pe.wait_ge(hT_ready, base + i + 1)
                    if base or second(i):
                        pe.wait_ge(hid_ready, DH * (base + i - 1))
                    for o in range(DH):
                        for k in range(DH):
                            ins = pe.matmul(ps_h[:, s, o, :], w_sb[:, a, k, o * P:(o + 1) * P], hT[:, s, k, :],
                                            start=(k == 0), stop=(k == DH - 1))
                        ins.then_inc(hid_done, 1)

                turn(0, 0)
                turn(1, 1)
                layer(0, 0, 0, 0)
                with pe.Fori(1, LAST // 2, 1) as i:
                    turn(2 * i, 0)
                    layer(2 * i - 1, 1, 0, 0)
                    turn(2 * i + 1, 1)
                    layer(2 * i, 0, 0, 0)
                turn(LAST, 0)
                layer(LAST - 1, 1, 0, 0)
                layer(LAST, 0, 0, 0)
                with pe.Fori(0, LAST // 2, 1) as i:
                    layer(2 * i, 1, 1, NCH)
                    layer(2 * i + 1, 0, 1, NCH)
                layer(LAST, 1, 1, NCH)

            @block.scalar
            def _(act):
                act.wait_ge(params_in, 16 * 2 * (1 + 3 * DH))

                def keep_turned(i, s):
                    act.wait_ge(turned, i + 1)
                    if second(i):
                        act.wait_ge(hid_done, DH * (i - 1))
                    act.activation(hT[:, s], ps_t[:, s], ACT.Copy).then_inc(hT_ready, 1)

                def keep_hidden(i, s, a, base):
                    for o in range(DH):
                        act.wait_ge(hid_done, DH * (base + i) + o + 1)
                        act.sem_inc(act_turn, 1)
                        act.activation(columns(i, o), ps_h[:, s, o, :], ACT.Identity,
                                       bias=vec[:, a, 0, o:o + 1]).then_inc(hid_ready, 1)

                def norm(i, s):
                    act.wait_ge(hid_done, DH * (NCH + i - 1))
                    act.sem_inc(act_turn, 1)
                    for k in range(DH):
                        ins = act.activation(hT[:, s, k, :], columns(i, k), ACT.Relu,
                                             scale=sc1[:, k:k + 1], bias=sh1[:, k:k + 1])
                    ins.then_inc(hT_ready, 1)

                keep_turned(0, 0)
                keep_turned(1, 1)
                keep_hidden(0, 0, 0, 0)
                with act.Fori(1, LAST // 2, 1) as i:
                    keep_turned(2 * i, 0)
                    keep_hidden(2 * i - 1, 1, 0, 0)
                    keep_turned(2 * i + 1, 1)
                    keep_hidden(2 * i, 0, 0, 0)
                keep_turned(LAST, 0)
                keep_hidden(LAST - 1, 1, 0, 0)
                keep_hidden(LAST, 0, 0, 0)
                act.wait_ge(var_ready, 1)
                act.activation(std[:], tmp[:], ACT.Sqrt).then_inc(std_ready, 1)
                act.wait_ge(norm_ready, 1)
                norm(0, 1)
                with act.Fori(0, LAST // 2, 1) as i:
                    norm(2 * i + 1, 0)
                    keep_hidden(2 * i, 1, 1, NCH)
                    norm(2 * i + 2, 1)
                    keep_hidden(2 * i + 1, 0, 1, NCH)
                keep_hidden(LAST, 1, 1, NCH)
                act.wait_ge(var_ready, 2)
                act.activation(std[:], tmp[:], ACT.Sqrt).then_inc(std_ready, 1)


def gate(nc, c, x, w1, b1, wg, bg, wd, hid, expert_w, scale, shift, regions, ends):
    with ExitStack() as ctx:
        m = Memory(nc, ctx, "gate")
        wg_sb = m.sb("wg_sb", [P, KC, NE])
        w_hi = m.sb("w_hi", [P, DH, HID], F32R)
        w_lo = m.sb("w_lo", [P, DH, HID], F32R)
        wg_parts = m.sb("wg_parts", [P, KC, 2 * NE], F32R)
        xnT_hi = m.sb("xnT_hi", [P, 2, DH, CN], F32R)
        xnT_lo = m.sb("xnT_lo", [P, 2, DH, CN], F32R)
        act_hi = m.sb("act_hi", [P, 2, CN], F32R)
        act_lo = m.sb("act_lo", [P, 2, CN], F32R)
        fold = m.sb("fold", [2 * NE, NE])
        b_sb = m.sb("b_sb", [P, KC])
        bg_sb = m.sb("bg_sb", [P, NE])
        turns = m.sb("turns", [P, CH * D])
        out2 = turns[:].rearrange("p (k n) -> p k n", k=DH)
        xn = turns[:].rearrange("p (j f) -> p j f", j=CH)
        xt = m.sb("xt", [P, CH, D])
        x2 = m.sb("x2", [P, 2, CH, D])
        act_h = m.sb("act_h", [P, 2, CN])
        pay = m.sb("pay", [P, 2, CH, PAY])
        w_in_pay = pay[:, 0].rearrange("p c f -> p (c f)")[:, 0:DH * HID].rearrange("p (k o) -> p k o", k=DH)
        stats = m.sb("stats", [P, CH, 6])
        mv = m.sb("mv", [P, CH, 2])
        rstd = m.sb("rstd", [P, CH, 1])
        var = m.sb("var", [P, CH, 1])
        half = m.sb("half", [P, CH])
        gT = m.sb("gT", [2 * NE, CN])
        logit = m.sb("logit", [P, CH, NE])
        best = m.sb("best", [P, CH])
        key = m.sb("key", [P, CH, NE])
        chosen = m.sb("chosen", [P, CH, NE])
        chosen16 = m.sb("chosen16", [P, CH, NE], BF16)
        token = m.sb("token", [P, CH])
        token_i = m.sb("token_i", [P, CH], I32)
        real = m.sb("real", [P, CH])
        stray = m.sb("stray", [P, CH])
        first = m.sb("first", [P, NE])
        first_i = m.sb("first_i", [P, NE], I32)
        sign_i = m.sb("sign_i", [P, NE], I32)
        sign = m.sb("sign", [P, NE])
        place = m.sb("place", [P, CH, NE])
        where = m.sb("where", [P, CH])
        where_i = m.sb("where_i", [P, 2, CH], I32)
        ps_x = m.ps("ps_x", [P, CH, D])
        ps_h = m.ps("ps_h", [P, 2, CN])
        ps_b = m.ps("ps_b", [P, 2, CH, P])
        ps_g = m.ps("ps_g", [P, 512])
        ps_p = m.ps("ps_p", [P, 512])
        ps_gate = ps_p[:, 256:256 + CH * NE].rearrange("p (j e) -> p j e", e=NE)
        ps_place = ps_p[:, 0:(CH + 1) * NE].rearrange("p (j e) -> p j e", e=NE)

        params_in = m.sem("params_in")
        iotas = m.sem("iotas")
        x_in = m.sem("x_in")
        w_in = m.sem("w_in")
        logit_sum = m.sem("logit_sum")
        logit_kept = m.sem("logit_kept")
        pe_turn = m.sem("pe_turn")
        out2_ready = m.sem("out2_ready")
        turned_back = m.sem("turned_back")
        residual_ready = m.sem("residual_ready")
        xn_ready = m.sem("xn_ready")
        xn_turned = m.sem("xn_turned")
        split = m.sem("split")
        xnT_hi_ready = m.sem("xnT_hi_ready")
        xnT_ready = m.sem("xnT_ready")
        h_done = m.sem("h_done")
        h_ready = m.sem("h_ready")
        act_lo_ready = m.sem("act_lo_ready")
        back_done = m.sem("back_done")
        back_ready = m.sem("back_ready")
        logit_done = m.sem("logit_done")
        chosen_ready = m.sem("chosen_ready")
        place_done = m.sem("place_done")
        where_ready = m.sem("where_ready")
        x2_copied = m.sem("x2_copied")
        sent = [m.sem(f"sent{s}") for s in range(2)]
        act_turn = m.sem("act_turn")
        pool_turn = m.sem("pool_turn")
        dve_turn = m.sem("dve_turn")
        steps_sem = m.sem("steps")
        PARAMS = 3 + KC

        def all_chunks(eng, chunk):
            chunk(0, 0, 0)
            chunk(1, 1, 0)
            with eng.Fori(1, LAST // 2, 1) as i:
                chunk(2 * i, 0, i)
                chunk(2 * i + 1, 1, i)
            chunk(LAST, 0, LAST // 2)

        def later(i, by=1):
            return not isinstance(i, int) or i >= by

        def is_last(i):
            return isinstance(i, int) and i == LAST

        with nc.Block() as block:

            @block.sync
            def _(sp):
                def load(i):
                    if later(i):
                        sp.wait_ge(residual_ready, i)
                    sp.dma_start(xt[:, 0, :], x[ds(i * CN, P), :]).then_inc(x_in, 16)
                    if is_last(i):
                        part = N - LAST * CN - P
                        sp.dma_start(xt[0:part, 1, :], x[N - part:N, :]).then_inc(x_in, 16)
                    else:
                        sp.dma_start(xt[:, 1:CH, :], x[ds(i * CN + P, CN - P), :].rearrange("(j p) f -> p j f", p=P)).then_inc(x_in, 16)

                load(0)
                sp.dma_start(w_in_pay, w1.rearrange("(k p) o -> p k o", p=P)).then_inc(params_in, 16)
                sp.dma_start(wg_sb[:], wg.rearrange("(k p) o -> p k o", p=P)).then_inc(params_in, 16)
                sp.dma_start(bg_sb[:], bg.partition_broadcast(P)).then_inc(params_in, 16)
                for k in range(KC):
                    sp.dma_start(b_sb[:, k:k + 1], b1[k * P:(k + 1) * P].rearrange("(p o) -> p o", o=1)).then_inc(params_in, 16)
                load(1)
                with sp.Fori(1, LAST // 2 - NE, 1) as i:
                    load(2 * i)
                    load(2 * i + 1)
                with sp.Fori(0, NE, 1) as e:
                    for u in range(2):
                        load(LAST - 2 * NE + 2 * e + u)
                    sp.wait_ge(out2_ready, 2 * e + 2)
                    sp.dma_start(expert_w[:, ds(e, 1), :, :].rearrange("p o k f -> p (o k) f"),
                                 wd.rearrange("e (k p) f -> p (e k) f", p=P)[:, ds(e * KC, KC), :]).then_inc(w_in, 16)
                load(LAST)
                sp.wait_ge(w_in, 16 * NE)

            @block.gpsimd
            def _(pool):
                pool.iota(token_i[:], [[P, CH]], base=0, channel_multiplier=1).then_inc(iotas, 1)
                pool.iota(first_i[:], [[CAP, PAIRS_E], [CAP - 1, 2]], base=0, channel_multiplier=0).then_inc(iotas, 1)
                pool.iota(sign_i[:], [[0, PAIRS_E], [-2, 2]], base=1, channel_multiplier=0).then_inc(iotas, 1)

                def send(i, s):
                    pool.wait_ge(where_ready, i + 1)
                    pool.wait_ge(x2_copied, i + 1)
                    pool.sem_inc(pool_turn, 1)
                    for j in range(CH):
                        pool.indirect_dma_start(
                            out=regions[:, :],
                            out_offset=bass.IndirectOffsetOnAxis(ap=where_i[:, s, j:j + 1], axis=0),
                            in_=pay[:, s, j, :], in_offset=None,
                        ).then_inc(sent[s], 16)

                def chunk(i, s, before):
                    if later(i):
                        send(i - 1, 1 - s)
                    if later(i, 2):
                        pool.wait_ge(sent[s], 16 * CH * before)
                    pool.wait_ge(residual_ready, i + 1)
                    pool.sem_inc(pool_turn, 1)
                    pool.tensor_copy(pay[:, s, :, PAY_X:PAY_X + D], x2[:, s]).then_inc(x2_copied, 1)

                all_chunks(pool, chunk)
                send(LAST, 0)
                for s in range(2):
                    pool.wait_ge(sent[s], 16 * CH * (LAST // 2 + 1 - s))

            @block.scalar
            def _(act):
                act.wait_ge(params_in, 16 * PARAMS)

                def second_output(i):
                    if later(i):
                        act.wait_ge(turned_back, i)
                        act.sem_inc(act_turn, 1)
                    for k in range(DH):
                        ins = act.activation(out2[:, k, :], hid[:, ds(i, 1), k, :].rearrange("p o n -> p (o n)"), ACT.Relu,
                                             scale=scale[:, k:k + 1], bias=shift[:, k:k + 1])
                    ins.then_inc(out2_ready, 1)

                def keep_xnT(i, s):
                    act.wait_ge(xn_turned, i + 1)
                    act.activation(xnT_hi[:, s], ps_x[:].rearrange("p c f -> p (c f)").rearrange("p (k n) -> p k n", k=DH),
                                   ACT.Copy).then_inc(xnT_hi_ready, 1)

                def keep_logits(i):
                    act.wait_ge(logit_sum, i + 1)
                    if later(i):
                        act.wait_ge(logit_done, i)
                        act.sem_inc(act_turn, 1)
                    act.activation(gT[:], ps_g[0:2 * NE, :], ACT.Copy).then_inc(logit_kept, 1)

                def chunk(i, s, before):
                    if not is_last(i):
                        second_output(i + 1)
                    for k in range(KC):
                        act.wait_ge(h_done, KC * i + k + 1)
                        act.sem_inc(act_turn, 1)
                        act.activation(act_h[:, k % 2, :], ps_h[:, k % 2, :], ACT.Gelu, bias=b_sb[:, k:k + 1])
                        act.activation(act_hi[:, k % 2, :], ps_h[:, k % 2, :], ACT.Gelu, bias=b_sb[:, k:k + 1]).then_inc(h_ready, 1)
                        if k == 0 and later(i):
                            keep_logits(i - 1)
                        if k == XN_AT and not is_last(i):
                            keep_xnT(i + 1, 1 - s)

                second_output(0)
                keep_xnT(0, 0)
                all_chunks(act, chunk)
                keep_logits(LAST)

            @block.vector
            def _(dve):
                steps = Steps(dve, steps_sem)
                steps.link(dve.tensor_tensor(fold[:], c.ident[0:2 * NE, 0:NE], c.ident[0:2 * NE, NE:2 * NE], ALU.add))
                dve.wait_ge(params_in, 16 * PARAMS)
                wg_hi, wg_lo = wg_parts[:, :, 0:NE], wg_parts[:, :, NE:2 * NE]
                steps.link(dve.tensor_copy(w_hi[:], w_in_pay))
                steps.link(dve.tensor_copy(wg_hi, wg_sb[:]))
                steps.link(dve.tensor_tensor(w_lo[:], w_in_pay, w_hi[:].bitcast(F32), ALU.subtract))
                steps.link(dve.tensor_tensor(wg_lo, wg_sb[:], wg_hi.bitcast(F32), ALU.subtract))
                dve.sem_inc(split, 1)
                dve.memset(pay[:, :, :, PAY_TOKEN:PAY], 0.0)
                dve.wait_ge(iotas, 3)
                steps.link(dve.tensor_copy(sign[:], sign_i[:]))
                steps.link(dve.tensor_copy(token[:], token_i[:]))
                steps.link(dve.tensor_scalar(stray[:], token[:], float(STRAY), None, ALU.add))
                steps.link(dve.tensor_copy(first[:], first_i[:]))
                wide = [P, CH, NE]

                def residual(i, s):
                    dve.wait_ge(x_in, 32 * (i + 1))
                    dve.wait_ge(turned_back, i + 1)
                    if later(i, 2):
                        dve.wait_ge(x2_copied, i - 1)
                    steps.link(dve.tensor_tensor(x2[:, s], xt[:], ps_x[:], ALU.add))
                    dve.sem_inc(residual_ready, 1)

                def moments(i, s):
                    for j in range(CH):
                        ins = dve.bn_stats(stats[:, j, :], x2[:, s, j, :])
                    steps.link(ins)
                    for j in range(CH):
                        ins = dve.bn_aggr(mv[:, j, :], stats[:, j, :])
                    steps.link(ins)
                    inverse_root(dve, steps, var[:, :, 0], rstd[:, :, 0], half[:], mv[:, :, 1])

                def normalise(i, s):
                    if later(i):
                        dve.wait_ge(xn_turned, i)
                    for j in range(CH):
                        ins = dve.tensor_scalar(xn[:, j, :], x2[:, s, j, :], mv[:, j, 0:1],
                                                rstd[:, j, 0:1], ALU.subtract, ALU.mult)
                    ins.then_inc(xn_ready, 1)

                def keep_xnT_rest(i, s):
                    dve.wait_ge(xnT_hi_ready, i + 1)
                    dve.sem_inc(dve_turn, 1)
                    dve.tensor_tensor(xnT_lo[:, s], ps_x[:].rearrange("p c f -> p (c f)").rearrange("p (k n) -> p k n", k=DH),
                                      xnT_hi[:, s].bitcast(F32), ALU.subtract).then_inc(xnT_ready, 1)

                def keep_rest(i, k):
                    dve.wait_ge(h_ready, KC * i + k + 1)
                    dve.sem_inc(dve_turn, 1)
                    dve.tensor_tensor(act_lo[:, k % 2, :], act_h[:, k % 2, :], act_hi[:, k % 2, :].bitcast(F32),
                                      ALU.subtract).then_inc(act_lo_ready, 1)

                def keep_back(i, s, k, before):
                    if k == 0 and later(i, 2):
                        dve.wait_ge(sent[s], 16 * CH * before)
                    dve.wait_ge(back_done, KC * i + k + 1)
                    dve.tensor_copy(pay[:, s, :, k * P:(k + 1) * P], ps_b[:, k % 2, :, :]).then_inc(back_ready, 1)

                def choose(i, s):
                    gates = pay[:, s, :, PAY_GATE:PAY_GATE + NE]
                    dve.wait_ge(logit_done, i + 1)
                    steps.link(dve.tensor_tensor(logit[:], ps_gate, bg_sb[:].unsqueeze(1).to_broadcast(wide), ALU.add))
                    steps.link(dve.tensor_reduce(best[:], logit[:], AX.X, ALU.max))
                    steps.link(dve.tensor_tensor(gates, logit[:], best[:].unsqueeze(2).to_broadcast(wide), ALU.subtract))
                    dve.tensor_copy(pay[:, s, :, PAY_TOKEN], token[:])
                    steps.link(dve.scalar_tensor_tensor(key[:], gates, 0.0, c.rev[:].unsqueeze(1).to_broadcast(wide),
                                                        ALU.is_ge, ALU.mult))
                    steps.link(dve.tensor_reduce(best[:], key[:], AX.X, ALU.max))
                    steps.link(dve.tensor_tensor(chosen[:], key[:], best[:].unsqueeze(2).to_broadcast(wide), ALU.is_equal))
                    if is_last(i):
                        steps.link(dve.tensor_scalar(real[:], token[:], float(N), None, ALU.is_lt))
                        steps.link(dve.tensor_tensor(chosen[:], chosen[:], real[:].unsqueeze(2).to_broadcast(wide), ALU.mult))
                    dve.tensor_tensor(chosen16[:], chosen[:], sign[:].unsqueeze(1).to_broadcast(wide), ALU.mult).then_inc(chosen_ready, 1)
                    steps.link(dve.tensor_scalar(token[:], token[:], float(CN), None, ALU.add))

                def find_places(i, s):
                    dve.wait_ge(place_done, i + 1)
                    steps.link(dve.tensor_tensor(place[:], ps_place[:, 0:CH, :], first[:].unsqueeze(1).to_broadcast(wide), ALU.add))
                    steps.link(dve.tensor_tensor(place[:], place[:], chosen[:], ALU.mult))
                    if is_last(i):
                        steps.link(dve.tensor_reduce(where[:], place[:], AX.X, ALU.add))
                        steps.link(dve.tensor_scalar(real[:], real[:], -1.0, 1.0, ALU.mult, ALU.add))
                        steps.link(dve.tensor_tensor(real[:], real[:], stray[:], ALU.mult))
                        steps.link(dve.tensor_tensor(where_i[:, s, :], where[:], real[:], ALU.add))
                    else:
                        steps.link(dve.tensor_reduce(where[:], place[:], AX.X, ALU.add))
                        steps.link(dve.tensor_copy(where_i[:, s, :], where[:]))
                    steps.link(dve.tensor_tensor(first[:], first[:], ps_place[:, CH, :], ALU.add))
                    dve.sem_inc(where_ready, 1)

                def chunk(i, s, before):
                    steps.restart()
                    for k in range(KC):
                        if k > 0:
                            keep_back(i, s, k - 1, before)
                        elif later(i):
                            keep_back(i - 1, 1 - s, KC - 1, None)
                        keep_rest(i, k)
                        if not is_last(i):
                            if k == RESIDUAL_AT:
                                residual(i + 1, 1 - s)
                            if k == MOMENTS_AT:
                                moments(i + 1, 1 - s)
                            if k == NORMALISE_AT:
                                normalise(i + 1, 1 - s)
                            if k == XN_AT:
                                keep_xnT_rest(i + 1, 1 - s)
                        if later(i):
                            if k == CHOOSE_AT:
                                choose(i - 1, 1 - s)
                            if k == PLACE_AT:
                                find_places(i - 1, 1 - s)

                steps.restart()
                residual(0, 0)
                moments(0, 0)
                normalise(0, 0)
                keep_xnT_rest(0, 0)
                all_chunks(dve, chunk)
                steps.restart()
                keep_back(LAST, 0, KC - 1, None)
                choose(LAST, 0)
                find_places(LAST, 0)
                steps.link(dve.tensor_scalar(sign[:], sign[:], 0.5 * (P - 1), -0.5 * (P - 1), ALU.mult, ALU.add))
                steps.link(dve.tensor_tensor(ends[:], first[:], sign[:], ALU.add))

            @block.tensor
            def _(pe):
                pe.wait_ge(split, 1)

                def turn_back(i):
                    pe.wait_ge(out2_ready, i + 1)
                    if later(i):
                        pe.wait_ge(xnT_ready, i)
                    for j in range(CH):
                        for k in range(DH):
                            ins = pe.transpose(ps_x[:, j, k * P:(k + 1) * P], out2[:, k, j * P:(j + 1) * P], c.ident[:])
                    ins.then_inc(turned_back, 1)

                def turn_xn(i):
                    pe.wait_ge(xn_ready, i + 1)
                    flat = ps_x[:].rearrange("p c f -> p (c f)")
                    for k in range(DH):
                        for j in range(CH):
                            ins = pe.transpose(flat[:, k * CN + j * P:k * CN + (j + 1) * P], xn[:, j, k * P:(k + 1) * P], c.ident[:])
                    ins.then_inc(xn_turned, 1)

                def back(i, k):
                    pe.wait_ge(h_ready, KC * i + k + 1)
                    if k >= 2 or later(i):
                        pe.wait_ge(back_ready, KC * i + k - 1)
                    for j in range(CH):
                        ins = pe.transpose(ps_b[:, k % 2, j, :], act_h[:, k % 2, j * P:(j + 1) * P], c.ident[:])
                    ins.then_inc(back_done, 1)

                def add_logits(i, k):
                    if k == 0 and later(i):
                        pe.wait_ge(logit_kept, i)
                    pe.wait_ge(act_lo_ready, KC * i + k + 1)
                    pe.sem_inc(pe_turn, 1)
                    pe.matmul(ps_g[0:2 * NE, :], wg_parts[:, k, :], act_hi[:, k % 2, :], start=(k == 0), stop=False)
                    ins = pe.matmul(ps_g[0:2 * NE, :], wg_parts[:, k, :], act_lo[:, k % 2, :], start=False, stop=(k == KC - 1))
                    if k == KC - 1:
                        ins.then_inc(logit_sum, 1)

                def turn_logits(i):
                    pe.wait_ge(logit_kept, i + 1)
                    if later(i):
                        pe.wait_ge(chosen_ready, i)
                        pe.wait_ge(where_ready, i)
                    pe.sem_inc(pe_turn, 1)
                    for j in range(CH):
                        ins = pe.matmul(ps_gate[:, j, :], gT[:, j * P:(j + 1) * P], fold[:], start=True, stop=True)
                    ins.then_inc(logit_done, 1)

                def count(i):
                    pe.wait_ge(chosen_ready, i + 1)
                    if later(i):
                        pe.wait_ge(where_ready, i)
                    for j in range(CH + 1):
                        for b in range(min(j, CH)):
                            ins = pe.matmul(ps_place[:, j, :], c.ones16[:], chosen16[:, b, :],
                                            start=(b == 0), stop=(j == CH and b == CH - 1))
                        if j < CH:
                            ins = pe.matmul(ps_place[:, j, :], c.after[:], chosen16[:, j, :], start=(j == 0), stop=True)
                    ins.then_inc(place_done, 1)

                def chunk(i, s, before):
                    for k in range(KC):
                        if k == 0:
                            pe.wait_ge(xnT_ready, i + 1)
                        if k >= 2 or later(i):
                            pe.wait_ge(h_ready, KC * i + k - 1)
                        for q in range(DH):
                            for w, a in ((w_hi, xnT_hi), (w_hi, xnT_lo), (w_lo, xnT_hi)):
                                ins = pe.matmul(ps_h[:, k % 2, :], w[:, q, k * P:(k + 1) * P], a[:, s, q, :],
                                                start=(q == 0 and w is w_hi and a is xnT_hi),
                                                stop=(q == DH - 1 and w is w_lo))
                        ins.then_inc(h_done, 1)
                        if k > 0:
                            back(i, k - 1)
                        elif later(i):
                            back(i - 1, KC - 1)
                        if k == TURN_LOGITS_AT and later(i):
                            turn_logits(i - 1)
                        if k == COUNT_AT and later(i):
                            count(i - 1)
                        if k == XN_AT and not is_last(i):
                            turn_xn(i + 1)
                        if k > 0:
                            add_logits(i, k - 1)
                        elif later(i):
                            add_logits(i - 1, KC - 1)
                        if k == 0 and not is_last(i):
                            turn_back(i + 1)

                turn_back(0)
                turn_xn(0)
                all_chunks(pe, chunk)
                back(LAST, KC - 1)
                add_logits(LAST, KC - 1)
                turn_logits(LAST)
                count(LAST)


def experts(nc, c, w_sb, bd, regions, ends, out):
    SLOTS = 6
    with ExitStack() as ctx:
        m = Memory(nc, ctx, "exp")
        w_lo = m.sb("w_lo", [P, NE, KC, D], F32R)
        b_sb = m.sb("b_sb", [P, NE, D])
        w_hi = m.sb("w_hi", [P, NE, KC, D], F32R)
        none = m.sb("none", [P, PAY])
        tile_i = m.sb("tile_i", [P, TTILES], I32)
        tile_f = m.sb("tile_f", [P, TTILES])
        past = m.sb("past", [P, TTILES])
        row = m.sb("row", [P, TTILES])
        expert = m.sb("expert", [P, TTILES])
        row_i = m.sb("row_i", [P, TTILES], I32)
        expert_i = m.sb("expert_i", [P, TTILES], I32)
        first = m.sb("first", [P, NE], I32)
        ntiles = m.sb("ntiles", [P, NE], I32)
        ntiles_f = m.sb("ntiles_f", [P, NE])
        cum = m.sb("cum", [P, NE])
        sign_i = m.sb("sign_i", [P, NE], I32)
        sign = m.sb("sign", [P, NE])
        offset = m.sb("offset", [P, NE])
        expd = m.sb("expd", [P, 2, NE])
        total = m.sb("total", [P, 2, 1])
        prob = m.sb("prob", [P, 2, 1])
        pay = m.sb("pay", [P, SLOTS, PAY])
        hT_hi = m.sb("hT_hi", [P, 2, KC, P], F32R)
        hT_lo = m.sb("hT_lo", [P, 2, KC, P], F32R)
        res = m.sb("res", [P, 2, D])
        token = m.sb("token", [P, 2, 1], I32)
        ps_t = m.ps("ps_t", [P, 2, KC, P])
        ps_y = m.ps("ps_y", [P, 2, 512])

        w_in = m.sem("w_in")
        iotas = m.sem("iotas")
        none_set = m.sem("none_set")
        none_out = m.sem("none_out")
        table_ready = m.sem("table_ready")
        pay_in = [m.sem(f"pay_in{s}") for s in range(SLOTS)]
        turned = m.sem("turned")
        w_hi_ready = m.sem("w_hi_ready")
        part_ready = m.sem("part_ready")
        w_split = m.sem("w_split")
        hT_hi_ready = m.sem("hT_hi_ready")
        hT_ready = m.sem("hT_ready")
        total_ready = m.sem("total_ready")
        y_done = m.sem("y_done")
        res_ready = m.sem("res_ready")
        out_done = [m.sem(f"out_done{s}") for s in range(2)]
        pool_turn = m.sem("pool_turn")
        dve_turn = m.sem("dve_turn")
        sp_turn = m.sem("sp_turn")
        steps_sem = m.sem("steps")
        U = SLOTS
        FULL = TTILES // U

        def half_of(w, n):
            return w[:, n // 2, ds(n % 2 * (KC // 2), KC // 2), :].rearrange("p k f -> p (k f)")

        def part(n):
            return hT_hi[:, n % 2].rearrange("p k q -> p (k q)")

        def all_tiles(eng, tile):
            for u in range(U):
                tile(u, u, 0)
            with eng.Fori(1, FULL, 1) as i:
                for u in range(U):
                    tile(U * i + u, u, i)
            for u in range(TTILES - U * FULL):
                tile(U * FULL + u, u, FULL)

        def later(i, by):
            return not isinstance(i, int) or i >= by

        with nc.Block() as block:

            @block.sync
            def _(sp):
                sp.wait_ge(none_set, 1)
                for e in range(NE):
                    end = sp.value_load(ends[0:1, e:e + 1], min_val=0, max_val=NOWHERE - P)
                    sp.dma_start(regions[ds(end, P), :], none[:]).then_inc(none_out, 16)
                sp.dma_start(regions[NOWHERE:NOWHERE + P, :], none[:]).then_inc(none_out, 16)
                sp.dma_start(b_sb[:].rearrange("p e f -> p (e f)"), bd.rearrange("e f -> (e f)").partition_broadcast(P)).then_inc(w_in, 16)
                sp.wait_ge(none_out, 16 * (NE + 1))
                sp.wait_ge(table_ready, 1)

                def tile(i, u, turn):
                    if later(i, SLOTS):
                        sp.wait_ge(res_ready, i - SLOTS + 1)
                        sp.sem_inc(sp_turn, 1)
                    at = sp.value_load(row_i[0:1, ds(i, 1)], min_val=0, max_val=NOWHERE)
                    sp.dma_start(pay[:, u % SLOTS, :], regions[ds(at, P), :]).then_inc(pay_in[u % SLOTS], 16)

                all_tiles(sp, tile)

            @block.gpsimd
            def _(pool):
                pool.iota(tile_i[:], [[1, TTILES]], base=0, channel_multiplier=0).then_inc(iotas, 1)
                pool.iota(first[:], [[CAP, PAIRS_E], [CAP - P, 2]], base=0, channel_multiplier=0).then_inc(iotas, 1)
                pool.iota(sign_i[:], [[0, PAIRS_E], [-2, 2]], base=1, channel_multiplier=0).then_inc(iotas, 1)

                def tile(i, u, turn):
                    pool.wait_ge(res_ready, i + 1)
                    pool.sem_inc(pool_turn, 1)
                    pool.indirect_dma_start(
                        out=out[:, :], out_offset=bass.IndirectOffsetOnAxis(ap=token[:, u % 2, :], axis=0),
                        in_=res[:, u % 2, :], in_offset=None, bounds_check=N - 1, oob_is_err=False,
                    ).then_inc(out_done[u % 2], 16)

                all_tiles(pool, tile)
                pool.wait_ge(out_done[0], 16 * ((TTILES + 1) // 2))
                pool.wait_ge(out_done[1], 16 * (TTILES // 2))

            @block.scalar
            def _(act):
                for e in range(NE):
                    act.activation(w_hi[:, e], w_sb[:, e], ACT.Copy).then_inc(w_hi_ready, 1)
                for n in range(2 * NE):
                    if n >= 2:
                        act.wait_ge(w_split, n - 1)
                    act.activation(part(n), half_of(w_sb, n), ACT.Copy).then_inc(part_ready, 1)

                def tile(i, u, turn):
                    s = u % 2
                    act.wait_ge(turned, i + 1)
                    if later(i, 2):
                        act.wait_ge(y_done, i - 1)
                    act.activation(hT_hi[:, s], ps_t[:, s], ACT.Copy).then_inc(hT_hi_ready, 1)
                    if later(i, 2):
                        act.wait_ge(res_ready, i - 1)
                    act.activation(expd[:, s, :], pay[:, u % SLOTS, PAY_GATE:PAY_GATE + NE], ACT.Exp,
                                   accum_out=total[:, s, :]).then_inc(total_ready, 1)

                all_tiles(act, tile)

            @block.vector
            def _(dve):
                steps = Steps(dve, steps_sem)
                steps.link(dve.memset(none[:], 0.0))
                dve.memset(none[:, PAY_TOKEN:PAY_TOKEN + 1], float(NO_TOKEN)).then_inc(none_set, 1)
                dve.wait_ge(iotas, 3)
                steps.link(dve.tensor_copy(sign[:], sign_i[:]))
                steps.link(dve.tensor_copy(tile_f[:], tile_i[:]))
                steps.link(dve.tensor_tensor(cum[:], ends[:], first[:], ALU.subtract))
                steps.link(dve.tensor_tensor(cum[:], cum[:], sign[:], ALU.mult))
                steps.link(dve.tensor_scalar(cum[:], cum[:], float(P - 1), None, ALU.add))
                steps.link(dve.tensor_copy(ntiles[:], cum[:]))
                steps.link(dve.tensor_scalar(ntiles[:], ntiles[:], 7, None, ALU.arith_shift_right))
                steps.link(dve.tensor_copy(ntiles_f[:], ntiles[:]))
                steps.link(dve.tensor_copy(cum[:], ntiles_f[:]))
                for e in range(1, NE):
                    steps.link(dve.tensor_tensor(cum[:, e:e + 1], cum[:, e:e + 1], cum[:, e - 1:e], ALU.add))
                steps.link(dve.tensor_tensor(offset[:], ntiles_f[:], cum[:], ALU.subtract))
                steps.link(dve.tensor_tensor(offset[:], offset[:], sign[:], ALU.mult))
                steps.link(dve.scalar_tensor_tensor(offset[:], offset[:], float(P), first[:], ALU.mult, ALU.add))
                steps.link(dve.memset(expert[:], 0.0))
                for e in range(NE):
                    steps.link(dve.scalar_tensor_tensor(expert[:], tile_f[:], cum[:, e:e + 1], expert[:], ALU.is_ge, ALU.add))
                steps.link(dve.tensor_scalar(row[:], expert[:], float(NE), float(NOWHERE), ALU.is_equal, ALU.mult))
                for e in range(NE):
                    way = float(P) if e % 2 == 0 else float(-P)
                    steps.link(dve.tensor_scalar(past[:], tile_f[:], way, offset[:, e:e + 1], ALU.mult, ALU.add))
                    steps.link(dve.scalar_tensor_tensor(past[:], expert[:], float(e), past[:], ALU.is_equal, ALU.mult))
                    steps.link(dve.tensor_tensor(row[:], row[:], past[:], ALU.add))
                steps.link(dve.tensor_copy(row_i[:], row[:]))
                steps.link(dve.tensor_scalar(expert_i[:], expert[:], float(NE - 1), None, ALU.min))
                dve.sem_inc(table_ready, 1)
                for n in range(2 * NE):
                    dve.wait_ge(part_ready, n + 1)
                    dve.tensor_tensor(half_of(w_lo, n), half_of(w_sb, n), part(n).bitcast(F32), ALU.subtract).then_inc(w_split, 1)
                dve.wait_ge(w_in, 16)
                dve.sem_inc(dve_turn, 1)

                def keep_rest(i, s):
                    dve.wait_ge(hT_hi_ready, i + 1)
                    if later(i, 2):
                        dve.wait_ge(y_done, i - 1)
                    dve.sem_inc(dve_turn, 1)
                    dve.tensor_tensor(hT_lo[:, s], ps_t[:, s], hT_hi[:, s].bitcast(F32), ALU.subtract).then_inc(hT_ready, 1)

                def tile(i, u, turn):
                    s = u % 2
                    steps.restart()
                    if not isinstance(i, int) or i + 1 < TTILES:
                        keep_rest(i + 1, 1 - s)
                    e = dve.value_load(expert_i[0:1, ds(i, 1)], min_val=0, max_val=NE - 1)
                    dve.wait_ge(y_done, i + 1)
                    if later(i, 2):
                        dve.wait_ge(out_done[s], 16 * (3 * turn + u // 2))
                    dve.sem_inc(dve_turn, 1)
                    steps.link(dve.tensor_tensor(res[:, s, :], ps_y[:, s, 0:D], b_sb[:, ds(e, 1), :].rearrange("p o f -> p (o f)"), ALU.add))
                    dve.tensor_copy(token[:, s, :], pay[:, u % SLOTS, PAY_TOKEN:PAY_TOKEN + 1])
                    dve.wait_ge(total_ready, i + 1)
                    dve.sem_inc(dve_turn, 1)
                    steps.link(dve.reciprocal(prob[:, s, :], total[:, s, :]))
                    dve.scalar_tensor_tensor(res[:, s, :], res[:, s, :], prob[:, s, :],
                                             pay[:, u % SLOTS, PAY_X:PAY_X + D], ALU.mult, ALU.add).then_inc(res_ready, 1)

                keep_rest(0, 0)
                all_tiles(dve, tile)

            @block.tensor
            def _(pe):
                pe.wait_ge(table_ready, 1)
                pe.wait_ge(w_hi_ready, NE)
                pe.wait_ge(w_split, 2 * NE)

                def turn_tile(i, u, turn):
                    s = u % 2
                    pe.wait_ge(pay_in[u % SLOTS], 16 * (turn + 1))
                    if later(i, 2):
                        pe.wait_ge(hT_ready, i - 1)
                    for k in range(KC):
                        ins = pe.transpose(ps_t[:, s, k, :], pay[:, u % SLOTS, k * P:(k + 1) * P], c.ident[:])
                    ins.then_inc(turned, 1)

                def multiply(i, s):
                    e = pe.value_load(expert_i[0:1, ds(i, 1)], min_val=0, max_val=NE - 1)
                    pe.wait_ge(hT_ready, i + 1)
                    if later(i, 2):
                        pe.wait_ge(res_ready, i - 1)
                    for k in range(KC):
                        for h, w in ((hT_hi, w_hi), (hT_hi, w_lo), (hT_lo, w_hi)):
                            ins = pe.matmul(ps_y[:, s, 0:D], h[:, s, k, :], w[:, ds(e, 1), k, :].rearrange("p o f -> p (o f)"),
                                            start=(k == 0 and h is hT_hi and w is w_hi), stop=(k == KC - 1 and h is hT_lo))
                    ins.then_inc(y_done, 1)

                turn_tile(0, 0, 0)
                for u in range(1, U):
                    turn_tile(u, u, 0)
                    multiply(u - 1, (u - 1) % 2)
                with pe.Fori(1, FULL, 1) as i:
                    for u in range(U):
                        turn_tile(U * i + u, u, i)
                        multiply(U * i + u - 1, (u - 1) % 2)
                for u in range(TTILES - U * FULL):
                    turn_tile(U * FULL + u, u, FULL)
                    multiply(U * FULL + u - 1, (u - 1) % 2)
                multiply(TTILES - 1, (TTILES - 1) % 2)


def gnn_ffn(nc, x, src, dst, edge_weight, gnn_eps, gnn_w1, gnn_b1, gnn_g1, gnn_be1, gnn_w2, gnn_b2, gnn_g2, gnn_be2,
            ffn_w1, ffn_b1, ffn_wg, ffn_bg, ffn_wd, ffn_bd, out):
    table = nc.dram_tensor("node_table", [ROWS, D], F32).ap()
    accs = [nc.dram_tensor(f"accumulator{k}", [ROWS, D], F32).ap() for k in range(STREAMS)]
    halves = nc.dram_tensor("target_halves", [2, ECOLS * P], BF16).ap()
    regions = nc.dram_tensor("regions", [REGION_ROWS, PAY], F32).ap()
    with ExitStack() as whole:
        m = Memory(nc, whole, "all")
        c = Constants(m)
        ends = m.sb("ends", [P, NE], I32)
        scale = m.sb("scale", [P, DH])
        shift = m.sb("shift", [P, DH])
        with ExitStack() as ctx:
            e = Memory(nc, ctx, "edges")
            edge_cols = e.sb("cols", [P, EGROUPS, 4, G])
            bases = e.sb("bases", [1, EGROUPS], I32)
            flag = e.sb("flag", [P, 1], I32)
            c.for_edges(e)
            prepare(nc, c, x, src, dst, edge_weight, gnn_eps, table, accs, halves, edge_cols, bases, flag)
            add_edges(nc, c, table, accs, halves, edge_cols, bases, flag)
        with ExitStack() as ctx:
            nodes = Memory(nc, ctx, "nodes").sb("hid", [P, NCH, DH, CN])
            hid = nodes[:]
            expert_w = hid.rearrange("p c h n -> p (c h n)")[:, 0:NE * KC * D].rearrange("p (e k f) -> p e k f", e=NE, k=KC)
            linear(nc, c, accs, gnn_w1, gnn_b1, gnn_g1, gnn_be1, gnn_w2, gnn_b2, gnn_g2, gnn_be2, hid, scale, shift)
            gate(nc, c, x, ffn_w1, ffn_b1, ffn_wg, ffn_bg, ffn_wd, hid, expert_w, scale, shift, regions, ends)
        experts(nc, c, expert_w, ffn_bd, regions, ends, out)


_INS = ['x', 'src', 'dst', 'edge_weight', 'L0_gnn_eps', 'L0_gnn_W1', 'L0_gnn_b1', 'L0_gnn_g1', 'L0_gnn_be1',
        'L0_gnn_W2', 'L0_gnn_b2', 'L0_gnn_g2', 'L0_gnn_be2', 'L0_ffn_W1', 'L0_ffn_b1', 'L0_ffn_Wg', 'L0_ffn_bg',
        'L0_ffn_Wd', 'L0_ffn_bd']


def kernel(**inputs):
    import numpy as _np
    import concourse.bacc as _bacc
    from concourse.bass_utils import run_bass_kernel_spmd as _run

    nc = _bacc.Bacc("TRN2", target_bir_lowering=False, num_devices=1)
    arrays, args = {}, []
    for name in _INS:
        a = _np.ascontiguousarray(inputs[name])
        arrays[f"in_{name}_dram"] = a
        args.append(nc.dram_tensor(f"in_{name}_dram", a.shape, mybir.dt.from_np(a.dtype), kind="ExternalInput").ap())
    args.append(nc.dram_tensor("out_0_dram", [N, D], F32, kind="ExternalOutput").ap())
    gnn_ffn(nc, *args)
    return _run(nc, [arrays], core_ids=[0]).results[0]["out_0_dram"]
```
